# Optimizing a Trainium2 kernel written in Bass

```python
import numpy as np
import jax
import jax.numpy as jnp

def _softmax(x, axis=-1):
    return jax.nn.softmax(x, axis=axis)

def _gelu(x):
    return jax.nn.gelu(x, approximate=True)

def _silu(x):
    return jax.nn.silu(x)

def _sigmoid(x):
    return jax.nn.sigmoid(x)

def _layernorm(x, axis=-1, eps=1e-05):
    m = jnp.mean(x, axis=axis, keepdims=True)
    v = jnp.var(x, axis=axis, keepdims=True)
    return (x - m) / jnp.sqrt(v + eps)

def _scatter_add(tgt, idx, src, axis=0):
    return tgt.at[idx].add(src)

def _segment_sum(src, seg, n):
    return jax.ops.segment_sum(src, seg, n)
kernel_name = 'mk_adaln_attn_ffn_d1_seqx_r4_575913'

def setup_inputs(seed: int=0):
    np.random.seed(seed)
    _w = jnp.asarray

    def _rec_inputs():
        import jax
        import jax.numpy as jnp
        _rk = jax.random.key(seed)
        x = -0.0001538 + 1 * jax.random.normal(jax.random.fold_in(_rk, 1), (16, 256, 256), jnp.float32)
        _lenS = 256 - jax.random.randint(jax.random.fold_in(_rk, 7), (16,), 0, max(1, 256 // 4) + 1, jnp.int32)
        _lenS2 = 256 - jax.random.randint(jax.random.fold_in(_rk, 8), (16,), 0, max(1, 256 // 4) + 1, jnp.int32)
        cond_1024 = 0.00782532 + 1.00527 * jax.random.normal(jax.random.fold_in(_rk, 11), (16, 256), jnp.float32)
        return (x, cond_1024)
    x, cond_1024 = _rec_inputs()

    def _L0_cond_setup():
        import jax, jax.numpy as jnp
        import numpy as np
        NUM_EXPERTS = 4
        TOP_K = 2
        key = jax.random.key(seed)
        ks = jax.random.split(key, 16)
        B, L, D, E, H = (8, 192, 256, NUM_EXPERTS, 1024)
        s = 0.02
        return {'context_c': jax.random.normal(ks[0], (B, L, D), jnp.float32), 'time_cond': jax.random.normal(ks[1], (B, D), jnp.float32), 'gate_w': jax.random.normal(ks[2], (3 * D, E), jnp.float32) * s, 'gate_b': jnp.zeros((E,), jnp.float32), 'time_w': jax.random.normal(ks[3], (D, 2 * E), jnp.float32) * s, 'time_b': jnp.zeros((2 * E,), jnp.float32), 'ew1': jax.random.normal(ks[4], (E, D, H), jnp.float32) * s, 'eb1': jnp.zeros((E, H), jnp.float32), 'ew2': jax.random.normal(ks[5], (E, H, D), jnp.float32) * s, 'eb2': jnp.zeros((E, D), jnp.float32), 'sw1': jax.random.normal(ks[6], (D, H), jnp.float32) * s, 'sb1': jnp.zeros((H,), jnp.float32), 'sw2': jax.random.normal(ks[7], (H, D), jnp.float32) * s, 'sb2': jnp.zeros((D,), jnp.float32)}
    _L0_cond_all = _L0_cond_setup()
    _L0_cond_in = {k: v for k, v in _L0_cond_all.items() if k in ('gate_w', 'gate_b', 'time_w', 'time_b', 'ew1', 'eb1', 'ew2', 'eb2', 'sw1', 'sb1', 'sw2', 'sb2')}
    del _L0_cond_all

    def _L0_attn_setup():
        import jax, jax.numpy as jnp
        import numpy as np
        DIM = 256
        NHEAD = 16
        HEAD_DIM = DIM // NHEAD

        def _rotate_half(t):
            h = t.shape[-1] // 2
            return jnp.concatenate([-t[..., h:], t[..., :h]], axis=-1)
        key = jax.random.key(seed)
        ks = jax.random.split(key, 5)
        B, N = (4, 512)
        return {'x': jax.random.normal(ks[0], (B, N, DIM), dtype=jnp.float32), 'qkv_w': jax.random.normal(ks[1], (3 * DIM, DIM), dtype=jnp.float32) * 0.02, 'qkv_b': jax.random.normal(ks[2], (3 * DIM,), dtype=jnp.float32) * 0.02, 'proj_w': jax.random.normal(ks[3], (DIM, DIM), dtype=jnp.float32) * 0.02, 'proj_b': jax.random.normal(ks[4], (DIM,), dtype=jnp.float32) * 0.02}
    _L0_attn_all = _L0_attn_setup()
    _L0_attn_in = {k: v for k, v in _L0_attn_all.items() if k in ('qkv_w', 'qkv_b', 'proj_w', 'proj_b')}
    del _L0_attn_all

    def _L0_cond2_setup():
        import jax, jax.numpy as jnp
        import numpy as np
        import math
        N, T, D, H = (64, 128, 256, 256)
        key = jax.random.key(seed)
        k1, k2, k3, k4 = jax.random.split(key, 4)
        x = jax.random.normal(k1, (N, T, D), dtype=jnp.float32)
        h0 = jax.random.normal(k2, (N, H), dtype=jnp.float32)
        Wx = jax.random.normal(k3, (D, 4 * H), dtype=jnp.float32) / math.sqrt(D)
        Wh = jax.random.normal(k4, (H, 4 * H), dtype=jnp.float32) / math.sqrt(H)
        b = jnp.zeros((4 * H,), dtype=jnp.float32)
        return {'x': x, 'h0': h0, 'Wx': Wx, 'Wh': Wh, 'b': b}
    _L0_cond2_all = _L0_cond2_setup()
    _L0_cond2_in = {k: v for k, v in _L0_cond2_all.items() if k in ('Wx', 'Wh', 'b')}
    del _L0_cond2_all

    def _L0_ffn_setup():
        import jax, jax.numpy as jnp
        import numpy as np
        B, T, D, R, E = (32, 256, 256, 64, 8)
        key = jax.random.key(seed)
        ks = jax.random.split(key, 12)
        inp = {}
        inp['x'] = jax.random.normal(ks[0], (B, T, D), dtype=jnp.float32)
        inp['base_W'] = jax.random.normal(ks[1], (D, D), dtype=jnp.float32) * (1.0 / np.sqrt(D))
        inp['base_b'] = jax.random.normal(ks[2], (D,), dtype=jnp.float32) * 0.01
        inp['disc_mu'] = jax.random.normal(ks[3], (E, D), dtype=jnp.float32) * 0.5
        inp['disc_sigma'] = jax.random.uniform(ks[4], (E, D), dtype=jnp.float32, minval=0.5, maxval=1.5)
        inp['down_W'] = jax.random.normal(ks[5], (E, D, R), dtype=jnp.float32) * (1.0 / np.sqrt(D))
        inp['down_b'] = jax.random.normal(ks[6], (E, R), dtype=jnp.float32) * 0.01
        inp['up_W'] = jax.random.normal(ks[7], (E, R, D), dtype=jnp.float32) * (1.0 / np.sqrt(R))
        inp['up_b'] = jax.random.normal(ks[8], (E, D), dtype=jnp.float32) * 0.01
        inp['conv_W'] = jax.random.normal(ks[9], (E, D, D), dtype=jnp.float32) * 0.02
        inp['conv_b'] = jax.random.normal(ks[10], (E, D), dtype=jnp.float32) * 0.01
        return inp
    _L0_ffn_all = _L0_ffn_setup()
    _L0_ffn_in = {k: v for k, v in _L0_ffn_all.items() if k in ('base_W', 'base_b', 'disc_mu', 'disc_sigma', 'down_W', 'down_b', 'up_W', 'up_b', 'conv_W', 'conv_b')}
    del _L0_ffn_all
    return {'x': x, 'cond_1024': cond_1024, 'L0_cond_gate_w': _L0_cond_in['gate_w'], 'L0_cond_gate_b': _L0_cond_in['gate_b'], 'L0_cond_time_w': _L0_cond_in['time_w'], 'L0_cond_time_b': _L0_cond_in['time_b'], 'L0_cond_ew1': _L0_cond_in['ew1'], 'L0_cond_eb1': _L0_cond_in['eb1'], 'L0_cond_ew2': _L0_cond_in['ew2'], 'L0_cond_eb2': _L0_cond_in['eb2'], 'L0_cond_sw1': _L0_cond_in['sw1'], 'L0_cond_sb1': _L0_cond_in['sb1'], 'L0_cond_sw2': _L0_cond_in['sw2'], 'L0_cond_sb2': _L0_cond_in['sb2'], 'L0_attn_qkv_w': _L0_attn_in['qkv_w'], 'L0_attn_qkv_b': _L0_attn_in['qkv_b'], 'L0_attn_proj_w': _L0_attn_in['proj_w'], 'L0_attn_proj_b': _L0_attn_in['proj_b'], 'L0_cond2_Wx': _L0_cond2_in['Wx'], 'L0_cond2_Wh': _L0_cond2_in['Wh'], 'L0_cond2_b': _L0_cond2_in['b'], 'L0_ffn_base_W': _L0_ffn_in['base_W'], 'L0_ffn_base_b': _L0_ffn_in['base_b'], 'L0_ffn_disc_mu': _L0_ffn_in['disc_mu'], 'L0_ffn_disc_sigma': _L0_ffn_in['disc_sigma'], 'L0_ffn_down_W': _L0_ffn_in['down_W'], 'L0_ffn_down_b': _L0_ffn_in['down_b'], 'L0_ffn_up_W': _L0_ffn_in['up_W'], 'L0_ffn_up_b': _L0_ffn_in['up_b'], 'L0_ffn_conv_W': _L0_ffn_in['conv_W'], 'L0_ffn_conv_b': _L0_ffn_in['conv_b']}

def reference(x, cond_1024, L0_cond_gate_w, L0_cond_gate_b, L0_cond_time_w, L0_cond_time_b, L0_cond_ew1, L0_cond_eb1, L0_cond_ew2, L0_cond_eb2, L0_cond_sw1, L0_cond_sb1, L0_cond_sw2, L0_cond_sb2, L0_attn_qkv_w, L0_attn_qkv_b, L0_attn_proj_w, L0_attn_proj_b, L0_cond2_Wx, L0_cond2_Wh, L0_cond2_b, L0_ffn_base_W, L0_ffn_base_b, L0_ffn_disc_mu, L0_ffn_disc_sigma, L0_ffn_down_W, L0_ffn_down_b, L0_ffn_up_W, L0_ffn_up_b, L0_ffn_conv_W, L0_ffn_conv_b):
    import jax
    import jax.numpy as jnp

    def _L0_cond_ref(context_c, time_cond, gate_w, gate_b, time_w, time_b, ew1, eb1, ew2, eb2, sw1, sb1, sw2, sb2):
        import jax, jax.numpy as jnp
        import numpy as np
        NUM_EXPERTS = 4
        TOP_K = 2
        B, L, D = context_c.shape
        E, K = (NUM_EXPERTS, TOP_K)
        L_head = L_wrist = L // 3
        head = context_c[:, :L_head]
        wrist = context_c[:, L_head:L_head + L_wrist]
        proprio = context_c[:, L_head + L_wrist:]
        full_agg = context_c.mean(axis=1)
        hp_agg = jnp.concatenate([head, proprio], axis=1).mean(axis=1)
        wp_agg = jnp.concatenate([wrist, proprio], axis=1).mean(axis=1)
        gate_in = jnp.concatenate([full_agg, hp_agg, wp_agg], axis=-1)
        gate_logits = gate_in @ gate_w + gate_b
        mod = jax.nn.silu(time_cond) @ time_w + time_b
        scale, shift = jnp.split(mod, 2, axis=-1)
        gate_logits = gate_logits * (1.0 + scale) + shift
        gate_scores = jax.nn.softmax(gate_logits, axis=-1)
        topk_w, topk_i = jax.lax.top_k(gate_scores, K)
        topk_w = topk_w / (topk_w.sum(axis=-1, keepdims=True) + 1e-08)
        onehot = (topk_i[..., None] == jnp.arange(E)[None, None, :]).astype(context_c.dtype)
        w_be = jnp.sum(topk_w[..., None] * onehot, axis=1)
        mask = np.ones((E, L), dtype=np.float32)
        mask[1, L_head:L_head + L_wrist] = 0.0
        mask[2, :L_head] = 0.0
        mask = jnp.asarray(mask)
        out = jnp.zeros_like(context_c)
        for e in range(E):
            h = jax.nn.gelu(context_c @ ew1[e] + eb1[e], approximate=True)
            y = h @ ew2[e] + eb2[e]
            out = out + w_be[:, e][:, None, None] * mask[e][None, :, None] * y
        shared = jax.nn.gelu(context_c @ sw1 + sb1, approximate=True) @ sw2 + sb2
        return out + shared

    def _L0_attn_ref(x, qkv_w, qkv_b, proj_w, proj_b):
        import jax, jax.numpy as jnp
        import numpy as np
        DIM = 256
        NHEAD = 16
        HEAD_DIM = DIM // NHEAD

        def _rotate_half(t):
            h = t.shape[-1] // 2
            return jnp.concatenate([-t[..., h:], t[..., :h]], axis=-1)
        B, N, D = x.shape
        H, hd = (NHEAD, HEAD_DIM)
        qkv = x @ qkv_w.T + qkv_b
        qkv = jnp.transpose(qkv.reshape(B, N, 3, H, hd), (2, 0, 3, 1, 4))
        q, k, v = (qkv[0], qkv[1], qkv[2])
        inv_freq = 1.0 / 10000.0 ** (jnp.arange(0, hd, 2, dtype=x.dtype) / hd)
        pos = jnp.arange(N, dtype=x.dtype)
        freqs = pos[:, None] * inv_freq[None, :]
        emb = jnp.concatenate([freqs, freqs], axis=-1)
        cos = jnp.cos(emb)[None, None, None]
        sin = jnp.sin(emb)[None, None, None]
        q = q * cos + _rotate_half(q) * sin
        k = k * cos + _rotate_half(k) * sin
        scale = hd ** (-0.5)
        attn = jnp.einsum('abhqd,abhkd->abhqk', q, k) * scale
        attn = jax.nn.softmax(attn, axis=-1)
        out = jnp.einsum('abhqk,bhkd->abhqd', attn, v)
        out = jnp.swapaxes(out, 1, 2).reshape(B, N, D)
        out = out @ proj_w.T + proj_b
        return out

    def _L0_cond2_ref(x, h0, Wx, Wh, b):
        import jax, jax.numpy as jnp
        import numpy as np
        import math
        N, T, D, H = (64, 128, 256, 256)
        Hdim = h0.shape[1]
        xW = jnp.einsum('ntd,dg->ntg', x, Wx) + b

        def step(carry, xw_t):
            prev_h, prev_c = carry
            a = xw_t + prev_h @ Wh
            i = jax.nn.sigmoid(a[:, :Hdim])
            f = jax.nn.sigmoid(a[:, Hdim:2 * Hdim])
            o = jax.nn.sigmoid(a[:, 2 * Hdim:3 * Hdim])
            g = jnp.tanh(a[:, 3 * Hdim:])
            next_c = f * prev_c + i * g
            next_h = o * jnp.tanh(next_c)
            return ((next_h, next_c), next_h)
        c0 = jnp.zeros_like(h0)
        _, hs = jax.lax.scan(step, (h0, c0), jnp.swapaxes(xW, 0, 1))
        return jnp.swapaxes(hs, 0, 1)

    def _L0_ffn_ref(x, base_W, base_b, disc_mu, disc_sigma, down_W, down_b, up_W, up_b, conv_W, conv_b):
        import jax, jax.numpy as jnp
        import numpy as np
        B, T, D, R, E = (32, 256, 256, 64, 8)
        base = jnp.einsum('btd,od->bto', x, base_W) + base_b
        m1 = x.mean(axis=1)
        m2 = (x * x).mean(axis=1)
        inv_var = 1.0 / (disc_sigma * disc_sigma)
        losses = (jnp.einsum('bd,ed->eb', m2, inv_var) - 2.0 * jnp.einsum('bd,ed->eb', m1, disc_mu * inv_var) + jnp.sum(disc_mu * disc_mu * inv_var, axis=1)[:, None]) / D
        idx = jnp.argmin(losses, axis=0)
        Wd, bd = (down_W[idx], down_b[idx])
        Wu, bu = (up_W[idx], up_b[idx])
        Wc, bc = (conv_W[idx], conv_b[idx])
        h = jax.nn.relu(jnp.einsum('btd,bdr->btr', x, Wd) + bd[:, None, :])
        a = jnp.einsum('btr,brd->btd', h, Wu) + bu[:, None, :]
        y = jnp.einsum('btd,bod->bto', a, Wc) + bc[:, None, :]
        return base + y
    x = x + _L0_attn_ref(_L0_cond_ref(x, cond_1024, L0_cond_gate_w, L0_cond_gate_b, L0_cond_time_w, L0_cond_time_b, L0_cond_ew1, L0_cond_eb1, L0_cond_ew2, L0_cond_eb2, L0_cond_sw1, L0_cond_sb1, L0_cond_sw2, L0_cond_sb2), L0_attn_qkv_w, L0_attn_qkv_b, L0_attn_proj_w, L0_attn_proj_b)
    x = x + _L0_ffn_ref(_L0_cond2_ref(x, cond_1024, L0_cond2_Wx, L0_cond2_Wh, L0_cond2_b), L0_ffn_base_W, L0_ffn_base_b, L0_ffn_disc_mu, L0_ffn_disc_sigma, L0_ffn_down_W, L0_ffn_down_b, L0_ffn_up_W, L0_ffn_up_b, L0_ffn_conv_W, L0_ffn_conv_b)
    return x

_drawn_inputs = setup_inputs


def setup_inputs(seed=0):
    import zlib

    import numpy as np

    out = dict(_drawn_inputs(seed))
    spreads = {'L0_cond_gate_b': (0.0, 0.8),
     'L0_cond_time_b': (0.0, 0.8),
     'L0_cond_eb1': (0.0, 0.8),
     'L0_cond_eb2': (0.0, 0.8),
     'L0_cond_sb1': (0.0, 0.8),
     'L0_cond_sb2': (0.0, 0.745),
     'L0_cond2_b': (0.0, 0.8)}
    factors = {'cond_1024': 4.363,
     'L0_cond_gate_w': 8.0,
     'L0_cond_time_w': 8.0,
     'L0_cond_ew1': 8.0,
     'L0_cond_ew2': 8.0,
     'L0_cond_sw1': 8.0,
     'L0_cond_sw2': 8.0,
     'L0_attn_qkv_w': 4.426,
     'L0_attn_qkv_b': 7.658,
     'L0_attn_proj_w': 3.878,
     'L0_attn_proj_b': 22.016,
     'L0_ffn_base_b': 200.0,
     'L0_ffn_down_b': 64.0,
     'L0_ffn_up_b': 64.0,
     'L0_ffn_conv_b': 200.0,
     'L0_cond2_Wx': 3.037,
     'L0_cond2_Wh': 8.0,
     'L0_ffn_base_W': 3.108,
     'L0_ffn_disc_mu': 8.0,
     'L0_ffn_disc_sigma': 8.0,
     'L0_ffn_down_W': 8.0,
     'L0_ffn_up_W': 8.0,
     'L0_ffn_conv_W': 8.0}
    for name, (base, spread) in spreads.items():
        noise = np.random.default_rng([zlib.crc32(name.encode()), seed]).standard_normal(out[name].shape)
        drawn = base * np.exp(spread * noise) if base else spread * noise
        out[name] = jnp.asarray(drawn.astype(out[name].dtype))
    for name, factor in factors.items():
        out[name] = (out[name] * factor).astype(out[name].dtype)
    return out
```

```python
from contextlib import ExitStack

import concourse.bass as bass
from concourse import mybir

ALU = mybir.AluOpType
ACT = mybir.ActivationFunctionType
AX = mybir.AxisListType
F32 = mybir.dt.float32
F16 = mybir.dt.float16
I32 = mybir.dt.int32

P = 128
WSCALE = 64.0
HEAD = 16
SLOT = 64
KSUM = 48
KMAX = 50


GATE_READY, LOGITS_READY, TABLE_READY, SETUP_DONE = 25, 30, 59, 84
STATS_READY, INDEX_READY = 1, 7
ROWS_CLEAR, ALL_FILLED = 3, 13


def match(flat, like):
    return flat if len(like.shape) == 2 else flat.rearrange("p (a n) -> p a n", a=like.shape[1])


def wait(engine, sem, value):
    if not (isinstance(value, int) and value <= 0):
        engine.wait_ge(sem, value)


def mixer_kernel(nc, d):
    B, T, D = 16, 256, 256
    KC = D // P
    TT = T // P
    HID = d["ew1"].shape[2]
    HC = HID // P
    E = d["ew1"].shape[0]
    NH = D // HEAD
    EF = d["convT"].shape[0]
    R = d["upT"].shape[3] - 1
    G4 = 4 * D
    GC = G4 // P
    W = KC * HID
    BIAS = HC + KC
    BLK = 4 * W + 2 * BIAS
    LH = T // 3
    SEGS = [(0, LH), (LH, 2 * LH), (2 * LH, T)]
    GROUPS = HC // 2
    SB = 4
    BODY = 2 * SB
    EB = 2 * KC * R + 2 * D + 2

    LT = T // B
    mixed = nc.dram_tensor("mixed", [T, D], F32, kind="Internal").ap()
    scratch = nc.dram_tensor("expert_blocks", [E, P, BLK], F16, kind="Internal").ap()

    with ExitStack() as ctx:
        def sb(name, shape, dt=F32):
            return ctx.enter_context(nc.sbuf_tensor(name, shape, dt))

        def sem(name):
            return ctx.enter_context(nc.semaphore(name))

        banks = [ctx.enter_context(nc.psum_tensor(f"bank{i}", [P, 512], F32)) for i in range(8)]
        l1_bank = banks[0:2]
        y_bank = banks[2]
        bA, bB, bC, bD, bE = banks[3:8]

        wsel = sb("wsel", [P, 2, BLK], F16)
        wshared = sb("wshared", [P, BLK], F16)
        x2h = sb("x2h", [P, KC, T, B], F16)
        x2l = sb("x2l", [P, KC, T, B], F16)
        lstm_w = sb("lstm_w", [P, 2, 2, KC * G4], F16)
        adapt = sb("adapt", [P, EF, EB], F16)
        base_w = sb("base_w", [P, 2, KC * D], F16)
        qkv_w = sb("qkv_w", [P, 2, KC * 3 * D], F16)
        proj_w = sb("proj_w", [P, 2, KC * D], F16)
        ident = sb("ident", [P, P])
        ident16 = sb("ident16", [P, P], F16)
        ident64 = sb("ident64", [P, P], F16)
        cos_t = sb("cos_t", [P, TT, 2, HEAD])
        sin_t = sb("sin_t", [P, TT, 2, HEAD])
        brow_q = sb("brow_q", [33, 3 * D], F16)
        brow_l = sb("brow_l", [33, G4], F16)
        ones33 = sb("ones33", [33, P], F16)
        pbias = sb("pbias", [P, KC])
        gates_b = sb("gates_b", [P, B, 8])
        idx_moe = sb("idx_moe", [1, B, 2], I32)
        idx_ffn = sb("idx_ffn", [1, B], I32)

        xt = sb("xt", [P, KC, T])
        xr = sb("xr", [P, KC, T])
        xs = sb("xs", [P, 2, KC, T], F16)
        hf = sb("hf", [P, 2, 2 * T])
        hh = sb("hh", [P, 2, HC, T], F16)
        acc = sb("acc", [P, KC, T])
        yb = sb("yb", [P, KC, T])
        cs = sb("cs", [P, 2, KC, T], F16)
        t1 = sb("t1", [P, 2 * D])
        t2 = sb("t2", [P, 2 * D])
        qkn = sb("qkn", [P, TT, 2 * NH, SLOT], F16)
        vp = sb("vp", [P, TT, NH, 32])
        kT = sb("kT", [P, NH // 2, T], F16)
        qT = sb("qT", [P, NH // 2, T], F16)
        big = sb("big", [P, 2 * 4 * KC * T])
        oT = sb("oT", [P, 4, T])
        an = sb("an", [P, TT, D])
        arow = sb("arow", [P, TT, D])
        ah = sb("ah", [P, 2, TT, D], F16)
        aT = sb("aT", [P, 2, KC, T], F16)
        xo = sb("xo", [P, KC, T])
        mneg = sb("mneg", [P, TT, NH])
        recs = sb("recs", [P, TT, NH])
        small = sb("small", [P, 448])

        probs = big[:].rearrange("p (b h k q) -> p b h k q", b=2, h=4, k=KC)

        def halves(t):
            return t[:, 0, :], t[:, 1, :]

        block = ctx.enter_context(nc.Block())

        whi, wlo = halves(lstm_w[:, 0]), halves(lstm_w[:, 1])
        chunks = []

        def block_parts(t):
            return [(t[:, 0:W], t[:, W:2 * W]), (t[:, 2 * W:3 * W], t[:, 3 * W:4 * W])]

        def rows(ap):
            return ap.rearrange("(c p) n -> p c n", p=P)

        for src, (hi, lo) in zip((d["sw1"], d["sw2"]), block_parts(wshared)):
            chunks.append((rows(src), hi, lo, None))
        for e in range(E):
            for n, (src, (hi, lo)) in enumerate(zip((d["ew1"][e], d["ew2"][e]), block_parts(wsel[:, e % 2, :]))):
                chunks.append((rows(src), hi, lo, e if n == 1 else None))
        chunks.append((rows(d["qkvT"]), qkv_w[:, 0, :], qkv_w[:, 1, :], None))
        chunks.append((rows(d["projT"]), proj_w[:, 0, :], proj_w[:, 1, :], None))
        chunks.append((rows(d["wx"]), whi[0], whi[1], None))
        chunks.append((rows(d["wh"]), wlo[0], wlo[1], None))
        chunks.append((rows(d["baseT"]), base_w[:, 0, :], base_w[:, 1, :], None))
        chunks.append((d["downT"], adapt[:, :, 0:KC * R], adapt[:, :, KC * R:2 * KC * R], None))
        NCH = len(chunks)
        def stage(i):
            src = chunks[i][0]
            n = 1
            for s in src.shape[1:]:
                n *= s
            flat = big[:, (i % 2) * W:(i % 2) * W + n]
            return flat

        def as_3d(flat, src):
            return flat.rearrange("p (c n) -> p c n", c=src.shape[1])

        s_stage = [sem("s_stage0"), sem("s_stage1")]
        s_hi = sem("s_hi")
        s_lo = sem("s_lo")
        s_blk = [sem("s_blk0"), sem("s_blk1")]
        s_bias = sem("s_bias")
        s_const = sem("s_const")
        s_gx = [sem("s_gx0"), sem("s_gx1")]
        s_gsum = sem("s_gsum")
        s_set = sem("s_set")
        s_gp = sem("s_gp")
        s_ga = sem("s_ga")
        s_idx = sem("s_idx")
        s_cw = sem("s_cw")
        s_cp = sem("s_cp")
        s_cd = sem("s_cd")
        s_pool = sem("s_pool")

        condt = small[:, 0:32].rearrange("p (c b) -> p c b", c=KC)
        silu = small[:, 32:64].rearrange("p (c b) -> p c b", c=KC)
        agg = small[:, 64:160].rearrange("p (g b) -> p g b", b=B)
        sums = small[:, 160:256].rearrange("p (s c b) -> p s c b", s=3, c=KC)
        gw = sb("gw", [P, 3 * KC, E])
        tw = sb("tw", [P, KC, 2 * E])
        grow = sb("grow", [16, 12])
        route = sb("route", [16, 160])
        table = sb("table", [16, B, 8])
        ones16 = sb("ones16", [16, P])
        unit = sb("unit", [P, 1], F16)
        mu = sb("mu", [P, KC, EF])
        sg = sb("sg", [P, KC, EF])
        iv = sb("iv", [P, KC, EF])
        mi2 = sb("mi2", [P, KC, EF])
        mmi = sb("mmi", [P, KC, EF])
        onesf = sb("onesf", [P, B])
        rev = sb("rev", [16, 8])
        cbrow = sb("cbrow", [65, D])
        upconv = oT[:].rearrange("p q t -> p (q t)")[:, 0:KC * (R + 1 + D)].rearrange("p (c n) -> p c n", c=KC)
        dbias = sb("dbias", [R, EF])

        consts = [
            (ident[:], d["ident"]), (cos_t[:], d["cos_t"]), (sin_t[:], d["sin_t"]), (pbias[:], d["pbias"]),
            (condt, d["condT"]), (gw[:], d["gw"]), (tw[:], d["tw"]),
            (grow[:], d["grow"].partition_broadcast(16)), (rev[:], d["rev"].partition_broadcast(16)),
            (mu[:], d["muT"]), (sg[:], d["sgT"]), (dbias[:], d["downbT"]),
            (wshared[:, 4 * W:].bitcast(F32), d["sbias"]),
            (t1[0:1, :], d["qb"][:, 0:512]), (t1[32:33, :], d["qb"][:, 0:512]),
            (t2[0:1, 0:256], d["qb"][:, 512:768]), (t2[32:33, 0:256], d["qb"][:, 512:768]),
            (hf[0:1, 0, :], d["lb"][:, 0:512]), (hf[0:1, 1, :], d["lb"][:, 512:1024]),
            (hf[32:33, 0, :], d["lb"][:, 0:512]), (hf[32:33, 1, :], d["lb"][:, 512:1024]),
        ]

        s_xt = sem("s_xt")
        s_xr = sem("s_xr")
        s_xs = sem("s_xs")
        s_xc = sem("s_xc")
        s_wsel = [sem("s_wsel0"), sem("s_wsel1")]
        s_l1 = sem("s_l1")
        s_gel = sem("s_gel")
        s_hh = sem("s_hh")
        s_hs = sem("s_hs")
        s_l2 = sem("s_l2")
        s_y = sem("s_y")
        s_acc = sem("s_acc")
        s_ch = sem("s_ch")
        s_cs = sem("s_cs")
        s_qkv = sem("s_qkv")
        s_v = sem("s_v")
        s_rp = sem("s_rp")
        s_qkn = sem("s_qkn")
        s_dup = sem("s_dup")
        s_tr = sem("s_tr")
        s_te = sem("s_te")
        s_sn = sem("s_sn")
        s_mx = sem("s_mx")
        s_mh = sem("s_mh")
        s_mn = sem("s_mn")
        s_st = sem("s_st")
        s_exp = sem("s_exp")
        s_pv = sem("s_pv")
        s_oe = sem("s_oe")
        s_on = sem("s_on")
        s_rc = sem("s_rc")
        s_an = sem("s_an")
        s_mo = sem("s_mo")
        s_mi = sem("s_mi")
        s_ah = sem("s_ah")
        s_as = sem("s_as")
        s_at = sem("s_at")
        s_ate = sem("s_ate")
        s_pp = sem("s_pp")
        s_pj = sem("s_pj")
        s_xa = sem("s_xa")
        s_xh = sem("s_xh")
        s_x2 = sem("s_x2")

        def plan(moe, att):
            moe_steps = []
            for j in range(3):
                moe_steps += [("L1", j, g) for g in range(GROUPS)]
                moe_steps += [("L2", j, p) for p in range(HC // 2)]
            if not att:
                return moe_steps
            att_steps = {
                0: [("QK", 0)], 1: [("QK", 1)], 2: [("V",)], 3: [("TK",)], 4: [("TQ", 0)],
                5: [("SN", range(0, 3))], 6: [("SN", range(3, 6))], 7: [("SN", range(6, 9))],
                8: [("SN", range(9, 12))], 9: [("SN", range(12, 14))], 10: [("SN", range(14, 16))],
                11: [("TQ", 1)], 12: [("ST", 0)], 13: [("ST", 1)], 14: [("ST", 2), ("PV", 0)],
                15: [("ST", 3)], 16: [("PV", 1)], 20: [("ST", 4)], 21: [("ST", 5)],
                22: [("ST", 6), ("PV", 2)], 23: [("ST", 7), ("PV", 3), ("ON",), ("AT",), ("PJ",)],
            }
            steps = []
            for n, m in enumerate(moe_steps):
                if moe:
                    steps.append(m)
                steps += att_steps.get(n, [])
            return steps

        def phases(engine, emit):
            emit(plan(True, False), 0, None)
            emit(plan(True, True), 1, 0)
            with engine.Fori(2, B) as b:
                emit(plan(True, True), b, b - 1)
            emit(plan(False, True), None, B - 1)

        hist = [wsel[:, n, 0:KC * B * T].rearrange("p (c b t) -> p c b t", c=KC, b=B) for n in range(2)]
        ifg_bank = [banks[n][:].rearrange("p (g t b) -> p g t b", g=GC, t=SB) for n in (0, 1)]
        o_bank = [banks[n][:].rearrange("p (g t b) -> p g t b", g=GC, t=SB) for n in (3, 4)]

        def gate_out(pair, g):
            if g in (4, 5):
                return o_bank[pair][:, g - 4]
            return ifg_bank[pair][:, g if g < 4 else g - 2]

        spare = hh[:].rearrange("p n c t -> p (n c t)").bitcast(F32)
        used = [0]

        def carve(*shape, dt=F32):
            n = 1
            for k in shape:
                n *= k
            words = n if dt == F32 else n // 2
            flat = spare[:, used[0]:used[0] + words]
            used[0] += words
            flat = flat if dt == F32 else flat.bitcast(F16)
            names = "abc"[:len(shape)]
            return flat.rearrange(f"p ({' '.join(names)}) -> p {' '.join(names)}", **dict(zip(names, shape)))

        hs_f = carve(BODY, KC, B)
        hs_hi = carve(BODY, KC, B, dt=F16)
        hs_lo = carve(BODY, KC, B, dt=F16)
        hsq = carve(BODY, KC, B)
        stat = carve(4, KC * B)
        sif = carve(4, B)
        gcell = carve(4, B)
        prod = carve(4, B)
        so = carve(KC, B)
        tc_ = carve(KC, B)
        hsel = carve(2, EB, dt=F16)
        rs_ = t1[0:R + 1, :].bitcast(F16).rearrange("p (n k t) -> p n k t", n=2, k=2)
        rl = big[0:R, 0:2 * T].rearrange("p (n t) -> p n t", n=2)
        obuf = big[:, 2 * T:2 * T + 2 * TT * D].rearrange("p (n t) -> p n t", n=2)

        s_h0 = sem("s_h0")
        s_if = sem("s_if")
        s_o = sem("s_o")
        s_sig = sem("s_sig")
        s_o_used = sem("s_o_used")
        s_pr = sem("s_pr")
        s_c = sem("s_c")
        s_tc = sem("s_tc")
        s_h = sem("s_h")
        s_hfull = sem("s_hfull")
        s_hl = sem("s_hl")
        s_stat = sem("s_stat")
        s_hist = sem("s_hist")
        s_fl = sem("s_fl")
        s_fd = sem("s_fd")
        s_fidx = sem("s_fidx")
        s_sel = sem("s_sel")
        s_dn = sem("s_dn")
        s_rl = sem("s_rl")
        s_rh = sem("s_rh")
        s_rs = sem("s_rs")
        s_fo = sem("s_fo")
        s_ob = sem("s_ob")
        s_out = [sem("s_out0"), sem("s_out1")]

        @block.sync
        def _(sp):
            def load_chunk(i):
                src = chunks[i][0]
                sp.dma_start(as_3d(stage(i), src), src).then_inc(s_stage[i % 2], 16)

            load_chunk(0)
            load_chunk(1)
            sp.wait_ge(s_pool, ROWS_CLEAR)
            for dst, src in consts:
                sp.dma_start(dst, src).then_inc(s_const, 16)
            for b in range(2):
                sp.dma_start((xt, xr)[b][:], d["xT"][b]).then_inc(s_gx[b], 16)
            done_blocks = 0
            for i in range(2, NCH):
                sp.wait_ge(s_hi, i - 1)
                sp.wait_ge(s_lo, i - 1)
                load_chunk(i)
                e = chunks[i - 2][3]
                if e is not None:
                    sp.dma_start(scratch[e][:, 0:4 * W], wsel[:, e % 2, 0:4 * W]).then_inc(s_blk[e % 2], 16)
                    sp.dma_start(scratch[e][:, 4 * W:].bitcast(F32), d["ebias"][e]).then_inc(s_bias, 16)
                if i < B:
                    sp.wait_ge(s_gsum, i - 1)
                    sp.dma_start((xt, xr)[i % 2][:], d["xT"][i]).then_inc(s_gx[i % 2], 16)
            for b in range(min(NCH, B), B):
                sp.wait_ge(s_gsum, b - 1)
                sp.dma_start((xt, xr)[b % 2][:], d["xT"][b]).then_inc(s_gx[b % 2], 16)
            for e in range(EF):
                if e >= 1:
                    sp.wait_ge(s_cp, e)
                sp.dma_start(upconv[:, :, 0:R + 1], d["upT"][e]).then_inc(s_cw, 16)
                sp.dma_start(upconv[:, :, R + 1:], d["convT"][e]).then_inc(s_cw, 16)
                if e >= 1:
                    sp.wait_ge(s_cd, 2 * e)
                sp.dma_start(cbrow[64:65, :], d["cb"][e:e + 1, :]).then_inc(s_cw, 16)
                sp.dma_start(xo[64:65, 0, :], d["bb"]).then_inc(s_cw, 16)
            for n in range(2):
                sp.wait_ge(s_blk[n], 16 * E // 2)
            sp.wait_ge(s_bias, 16 * E)
            sp.wait_ge(s_gsum, B)
            sp.wait_ge(s_idx, 1)

            def moe_loads(b):
                wait(sp, s_xs, b)
                sp.dma_start(xt[:], d["xT"][bass.ds(b, 1)].rearrange("o p c t -> (o p) c t")).then_inc(s_xt, 16)
                for j in range(2):
                    if not (isinstance(b, int) and b == 0):
                        sp.wait_ge(s_y, 3 * b + j - 1)
                    e = sp.value_load(idx_moe[0:1, bass.ds(b, 1), j], min_val=0, max_val=E - 1)
                    sp.dma_start(wsel[:, j, :].bitcast(I32), scratch.bitcast(I32)[bass.ds(e, 1)].rearrange("o p n -> (o p) n")
                                 ).then_inc(s_wsel[j], 16)

            def att_loads(a):
                wait(sp, s_xa, a)
                sp.dma_start(xr[:], d["xL"][bass.ds(a, 1)].rearrange("o p c t -> (o p) c t")).then_inc(s_xr, 16)
                sp.wait_ge(s_an, 2 * a + 2)
                sp.dma_start(mixed.rearrange("(t p) n -> p t n", p=P), an[:]).then_inc(s_mo, 16)
                sp.wait_ge(s_mo, 16 * a + 16)
                wait(sp, s_as, a)
                for tt in range(TT):
                    src = mixed[tt * P:(tt + 1) * P, :].rearrange("(t r) (h e) -> t h r e", r=LT, e=HEAD)
                    for t in range(P // LT):
                        sp.dma_start(arow[t * B:(t + 1) * B, tt, :].rearrange("h (r e) -> h r e", e=HEAD), src[t]
                                     ).then_inc(s_mi, 16)

            moe_loads(0)
            moe_loads(1)
            att_loads(0)
            with sp.Fori(2, B) as b:
                moe_loads(b)
                att_loads(b - 1)
            att_loads(B - 1)

            with sp.Fori(0, B // 2) as i:
                for n in range(2):
                    sp.wait_ge(s_ob, 2 * i + n + 1)
                    dst = d["out"][bass.ds(2 * i + n, 1)].rearrange("o (t p) n -> (o p) t n", p=P)
                    sp.dma_start(dst, obuf[:, n, :].rearrange("p (t n) -> p t n", t=TT)).then_inc(s_out[n], 16)
            for n in range(2):
                sp.wait_ge(s_out[n], 16 * (B // 2))

        @block.gpsimd
        def _(pool):
            cleared = [0]

            def fill(ap, value):
                cleared[0] += 1
                nc.gpsimd.memset(ap, value).then_inc(s_pool, 1)
                pool.wait_ge(s_pool, cleared[0])

            for t in (t1[0:33, :], t2[0:33, :], hf[0:33]):
                fill(t, 0.0)
            assert cleared[0] == ROWS_CLEAR
            for t in (ones33, qkn, vp):
                fill(t[:], 0.0)
            fill(ones16[:], 1.0)
            fill(unit[:], 1.0)
            fill(onesf[:], 1.0)
            fill(ones33[0:1, :], 1.0)
            fill(ones33[32:33, :], 1.0)
            fill(vp[:, :, :, HEAD:HEAD + 1], WSCALE)
            fill(qkn[:, :, NH:2 * NH, KSUM:KMAX], 1.0)
            assert cleared[0] == ALL_FILLED

            def copy(out, in_):
                one = unit[:]
                while len(one.shape) < len(in_.shape):
                    one = one.unsqueeze(2)
                return nc.gpsimd.tensor_tensor(out, in_, one.to_broadcast(list(in_.shape)), ALU.mult)

            def att(a):
                for tt in range(TT):
                    pool.wait_ge(s_rp, 10 * a + 5 * tt + 5)
                    copy(qkn[:, tt, 0:NH, 32:48], qkn[:, tt, 0:NH, 0:16])
                    copy(qkn[:, tt, NH:2 * NH, 16:32], qkn[:, tt, NH:2 * NH, 0:16]).then_inc(s_dup, 1)

            with pool.Fori(0, B) as a:
                att(a)
            with pool.Fori(0, T // BODY) as i:
                pool.wait_ge(s_hl, BODY * i + BODY + 1)
                pool.wait_ge(s_x2, B)
                for n, src in enumerate((hs_hi, hs_lo)):
                    cp = copy(hist[n][:, :, :, bass.ds(BODY * i, BODY)],
                                               src[:].rearrange("p t c b -> p c b t"))
                cp.then_inc(s_hist, 1)

        @block.tensor
        def _(pe):
            mm = nc.tensor.matmul

            pe.wait_ge(s_pool, ALL_FILLED)
            pe.wait_ge(s_const, 16 * len(consts))
            pe.wait_ge(s_set, GATE_READY)
            for g in range(3 * KC):
                mm(bA[0:B, 0:E], agg[:, g, :], gw[:, g, :], start=(g == 0), stop=(g == 3 * KC - 1))
            for c in range(KC):
                m = mm(bB[0:B, 0:2 * E], silu[:, c, :], tw[:, c, :], start=(c == 0), stop=(c == KC - 1))
            m.then_inc(s_gp, 1)
            pe.wait_ge(s_set, TABLE_READY)
            mm(bC[:, 0:B * 8], ones16[:], table[:].rearrange("p b n -> p (b n)"), start=True, stop=True
               ).then_inc(s_gp, 1)
            for e in range(EF):
                pe.wait_ge(s_cw, 64 * (e + 1))
                if e >= 1:
                    pe.wait_ge(s_cd, 2 * e)
                for c in range(KC):
                    m = mm(bD[0:R + 1, 0:D], upconv[:, c, 0:R + 1], upconv[:, c, R + 1:], start=(c == 0),
                           stop=(c == KC - 1))
                m.then_inc(s_cp, 1)
            pe.wait_ge(s_hi, NCH)
            pe.wait_ge(s_lo, NCH)
            pe.wait_ge(s_set, SETUP_DONE)
            pe.wait_ge(s_pool, ALL_FILLED)

            THREE = ((0, 0), (1, 0), (0, 1))

            def moe(step, b):
                _, j, g = step
                blk = wshared[:] if j == 0 else wsel[:, j - 1, :]
                w1 = [blk[:, n * W:(n + 1) * W].rearrange("p (c n) -> p c n", c=KC) for n in range(2)]
                w2 = [blk[:, (2 + n) * W:(3 + n) * W].rearrange("p (c n) -> p c n", c=HC) for n in range(2)]
                if step[0] == "L1":
                    n = 12 * b + 4 * j + g
                    if j == 0 and g == 0:
                        pe.wait_ge(s_xs, b + 1)
                    if j >= 1 and g == 0:
                        pe.wait_ge(s_wsel[j - 1], 16 * b + 16)
                    wait(pe, s_gel, n - 1)
                    bank = l1_bank[g % 2]
                    for m in range(2):
                        ch = 2 * g + m
                        for k, (wp, xp) in enumerate(THREE):
                            for c in range(KC):
                                ins = mm(bank[:, m * T:(m + 1) * T], w1[wp][:, c, ch * P:(ch + 1) * P],
                                         xs[:, xp, c, :], start=(m == 0 and k == 0 and c == 0),
                                         stop=(k == 2 and c == KC - 1), skip_group_check=True)
                    ins.then_inc(s_l1, 1)
                else:
                    u = 3 * b + j
                    if g == 0:
                        wait(pe, s_y, u)
                    pe.wait_ge(s_hs, 4 * u + g + 1)
                    for ch in (2 * g, 2 * g + 1):
                        for k, (wp, hp) in enumerate(THREE):
                            for m in range(KC):
                                ins = mm(y_bank[:, m * T:(m + 1) * T], w2[wp][:, ch, m * P:(m + 1) * P],
                                         hh[:, hp, ch, :], start=(ch == 0 and k == 0 and m == 0),
                                         stop=(ch == HC - 1 and k == 2), skip_group_check=True)
                    if g == HC // 2 - 1:
                        ins.then_inc(s_l2, 1)

            def qk_or_v(a, tt, cols, bank, off, n, start):
                for k, (wp, cp) in enumerate(THREE):
                    for c in range(KC):
                        w = qkv_w[:, wp, :].rearrange("p (c n) -> p c n", c=KC)[:, c, cols:cols + n]
                        mm(bank[:, off:off + n], cs[:, cp, c, tt * P:(tt + 1) * P], w,
                           start=(start and k == 0 and c == 0), stop=False, skip_group_check=True)
                return mm(bank[:, off:off + n], ones33[:, :], brow_q[:, cols:cols + n], start=False, stop=True,
                          skip_group_check=True)

            def head_rows(h, k):
                lo = SLOT * (h % 2)
                return slice(lo, lo + k)

            def att(step, a):
                kind = step[0]
                if kind == "QK":
                    tt = step[1]
                    if tt == 0:
                        pe.wait_ge(s_cs, a + 1)
                        wait(pe, s_an, 2 * a)
                    qk_or_v(a, tt, 0, (bA, bB)[tt], 0, 2 * D, True).then_inc(s_qkv, 1)
                elif kind == "V":
                    wait(pe, s_ate, a)
                    for tt in range(TT):
                        ins = qk_or_v(a, tt, 2 * D, bC, tt * D, D, tt == 0)
                    ins.then_inc(s_qkv, 1)
                elif kind == "TK" or kind == "TQ":
                    is_k = kind == "TK"
                    if is_k:
                        pe.wait_ge(s_qkn, 2 * a + 2)
                        pe.wait_ge(s_dup, 2 * a + 2)
                        wait(pe, s_pj, a)
                        wait(pe, s_oe, 2 * a)
                    elif step[1] == 1:
                        pe.wait_ge(s_mn, a + 1)
                        pe.wait_ge(s_te, 6 * a + 4)
                    for half in range(2):
                        bank = ((bD, bE) if is_k else (bA, bB))[half]
                        out = bank[:].bitcast(F16).rearrange("p (g t) -> p g t", g=4)
                        for g in range(4):
                            h0 = (NH if is_k else 0) + 2 * (4 * half + g)
                            for tt in range(TT):
                                ins = nc.tensor.transpose(out[:, g, tt * P:(tt + 1) * P],
                                                          qkn[:, tt, h0:h0 + 2, :].rearrange("p h s -> p (h s)"),
                                                          ident16[:])
                        ins.then_inc(s_tr, 1)
                elif kind == "SN":
                    for h in step[1]:
                        if h == 0:
                            pe.wait_ge(s_te, 6 * a + 4)
                            pe.wait_ge(s_v, a + 1)
                        if h >= 3:
                            pe.wait_ge(s_mx, 16 * a + h - 2)
                        bank = (bC, bD, bE)[h % 3]
                        r = head_rows(h, KSUM)
                        for tt in range(TT):
                            ins = mm(bank[:, tt * T:(tt + 1) * T], qT[r, h // 2, tt * P:(tt + 1) * P],
                                     kT[r, h // 2, :], start=(tt == 0), stop=True, skip_group_check=True)
                        ins.then_inc(s_sn, 1)
                elif kind == "ST":
                    pair = step[1]
                    if pair == 0:
                        pe.wait_ge(s_te, 6 * a + 6)
                    if pair >= 2:
                        pe.wait_ge(s_exp, 8 * a + pair - 1)
                    for n in range(2):
                        h = 2 * pair + n
                        bank = ((bA, bB), (bC, bD))[pair % 2][n]
                        r = head_rows(h, KMAX)
                        for k in range(TT):
                            ins = mm(bank[:, k * T:(k + 1) * T], kT[r, h // 2, k * P:(k + 1) * P],
                                     qT[r, h // 2, :], start=(k == 0), stop=True, skip_group_check=True)
                    ins.then_inc(s_st, 1)
                elif kind == "PV":
                    q = step[1]
                    pe.wait_ge(s_exp, 8 * a + 2 * q + 2)
                    if q >= 2:
                        pe.wait_ge(s_oe, 2 * a + 1)
                    for k in range(TT):
                        for j in range(4):
                            ins = mm(bE[32 * j:32 * j + 32, (q % 2) * T:(q % 2 + 1) * T], vp[:, k, 4 * q + j, :],
                                     probs[:, q % 2, j, k, :], start=(k == 0), stop=(k == TT - 1),
                                     skip_group_check=True)
                    ins.then_inc(s_pv, 1)
                elif kind == "ON":
                    pe.wait_ge(s_oe, 2 * a + 2)
                    pe.wait_ge(s_exp, 8 * a + 8)
                    for tt in range(TT):
                        for q in range(4):
                            ins = nc.tensor.transpose((bA, bB)[tt][:, q * P:(q + 1) * P],
                                                      oT[:, q, tt * P:(tt + 1) * P], ident[:])
                        ins.then_inc(s_on, 1)
                elif kind == "AT":
                    pe.wait_ge(s_as, a + 1)
                    out = bC[:].bitcast(F16).rearrange("p (n c t) -> p n c t", n=2, c=KC)
                    for n in range(2):
                        for c in range(KC):
                            for tt in range(TT):
                                ins = nc.tensor.transpose(out[:, n, c, tt * P:(tt + 1) * P],
                                                          ah[:, n, tt, c * P:(c + 1) * P], ident16[:])
                    ins.then_inc(s_at, 1)
                elif kind == "PJ":
                    pe.wait_ge(s_ate, a + 1)
                    for m in range(KC):
                        for k, (wp, ap) in enumerate(THREE):
                            for c in range(KC):
                                w = proj_w[:, wp, :].rearrange("p (c n) -> p c n", c=KC)[:, c, m * P:(m + 1) * P]
                                ins = mm(bD[:, m * T:(m + 1) * T], w, aT[:, ap, c, :],
                                         start=(m == 0 and k == 0 and c == 0), stop=(k == 2 and c == KC - 1),
                                         skip_group_check=True)
                    ins.then_inc(s_pp, 1)

            def emit(steps, b, a):
                for step in steps:
                    if step[0] in ("L1", "L2"):
                        moe(step, b)
                    else:
                        att(step, a)

            phases(pe, emit)

            wl = [[lstm_w[:, s, n, :].rearrange("p (c n) -> p c n", c=KC) for n in range(2)] for s in range(2)]
            ORDER = (0, 1, 2, 3, 6, 7, 4, 5)

            def xw_part(n, pair, t0):
                for g in (2 * n, 2 * n + 1):
                    out = gate_out(pair, g).rearrange("p t b -> p (t b)")
                    mm(out, brow_l[:, g * P:(g + 1) * P], ones33[:, 0:SB * B], start=(g in (0, 4)), stop=False,
                       skip_group_check=True)
                    for wp, xp in THREE:
                        for c in range(KC):
                            src = (x2h, x2l)[xp][:, c, bass.ds(t0, SB), :].rearrange("p t b -> p (t b)")
                            ins = mm(out, wl[0][wp][:, c, g * P:(g + 1) * P], src, start=False, stop=False,
                                     skip_group_check=True)
                return ins

            pe.wait_ge(s_x2, B)
            for n in range(4):
                xw_part(n, 0, 0)

            def lstm_step(t, s, last_block):
                pair = s // SB
                prev = (s - 1) % BODY
                pe.wait_ge(s_h, t + 1)
                for g in ORDER:
                    for wp in range(2):
                        for c in range(KC):
                            mm(gate_out(pair, g)[:, s % SB, :], wl[1][wp][:, c, g * P:(g + 1) * P], hs_hi[:, prev, c, :],
                               start=False, stop=False, skip_group_check=True)
                pe.wait_ge(s_hl, t + 1)
                for g in ORDER:
                    for c in range(KC):
                        ins = mm(gate_out(pair, g)[:, s % SB, :], wl[1][0][:, c, g * P:(g + 1) * P], hs_lo[:, prev, c, :],
                                 start=False, stop=True, skip_group_check=True)
                    if g == 7:
                        ins.then_inc(s_if, 1)
                ins.then_inc(s_o, 1)

            def lstm_body(i, last):
                for s in range(BODY):
                    t = BODY * i + s
                    lstm_step(t, s, last)
                    if last and s >= SB:
                        continue
                    t0 = BODY * i + SB * (s // SB) + SB
                    xw_part(s % SB, 1 - s // SB, t0)

            lstm_body(0, False)
            with pe.Fori(1, T // BODY - 1) as i:
                lstm_body(i, False)
            lstm_body(T // BODY - 1, True)

            pe.wait_ge(s_fd, STATS_READY)
            k = 0
            st = stat[:].rearrange("p n (c b) -> p n c b", c=KC)
            for lhs, rhs in ((st[:, 3], iv), (st[:, 2], mi2), (None, mmi)):
                for c in range(KC):
                    ins = mm(bA[0:B, 0:EF], onesf[:] if lhs is None else lhs[:, c, :], rhs[:, c, :],
                             start=(k == 0), stop=(k == 5))
                    k += 1
            ins.then_inc(s_fl, 1)
            pe.wait_ge(s_fd, INDEX_READY)
            mm(bB[0:1, 0:B], route[:, 24:25], ident[0:B, 0:B], start=True, stop=True).then_inc(s_fl, 1)

            def ffn(b, n):
                down = [hsel[:, n, k * KC * R:(k + 1) * KC * R].rearrange("p (c r) -> p c r", c=KC) for k in range(2)]
                fold = [hsel[0:R + 1, n, 2 * KC * R + k * D:2 * KC * R + (k + 1) * D] for k in range(2)]
                bw = [base_w[:, k, :].rearrange("p (c n) -> p c n", c=KC) for k in range(2)]
                pe.wait_ge(s_sel, b + 1)
                for k, (wp, hp) in enumerate(THREE):
                    for c in range(KC):
                        rhs = hist[hp][:, c, bass.ds(b, 1), :].rearrange("p o t -> p (o t)")
                        ins = mm(banks[n][0:R, 0:T], down[wp][:, c, :], rhs, start=(k == 0 and c == 0),
                                 stop=(k == 2 and c == KC - 1), skip_group_check=True)
                ins.then_inc(s_dn, 1)
                out = banks[4 + n]
                for tt in range(TT):
                    cols = slice(tt * D, (tt + 1) * D)
                    first = tt == 0
                    for k, (wp, hp) in enumerate(THREE):
                        for c in range(KC):
                            lhs = hist[hp][:, c, bass.ds(b, 1), tt * P:(tt + 1) * P].rearrange("p o t -> p (o t)")
                            mm(out[:, cols], lhs, bw[wp][:, c, :], start=first, stop=False, skip_group_check=True)
                            first = False
                    for hp, x2 in enumerate((x2h, x2l)):
                        for c in range(KC):
                            lhs = x2[:, c, tt * P:(tt + 1) * P, bass.ds(b, 1)].rearrange("p t o -> p (t o)")
                            mm(out[:, tt * D + c * P:tt * D + (c + 1) * P], lhs, ident64[:], start=False, stop=False,
                               skip_group_check=True)
                pe.wait_ge(s_rs, b + 1)
                for tt in range(TT):
                    for k, (wp, hp) in enumerate(THREE):
                        ins = mm(out[:, tt * D:(tt + 1) * D], rs_[:, n, hp, tt * P:(tt + 1) * P], fold[wp],
                                 start=False, stop=(k == 2), skip_group_check=True)
                ins.then_inc(s_fo, 1)

            pe.wait_ge(s_hist, T // BODY)
            def adapter_body(i):
                for n in range(2):
                    wait(pe, s_ob, 2 * i)
                    ffn(2 * i + n, n)

            adapter_body(0)
            with pe.Fori(1, B // 2) as i:
                adapter_body(i)

        @block.scalar
        def _(act):
            A = nc.scalar.activation
            UN = 1.0 / WSCALE
            for i in range(NCH):
                act.wait_ge(s_stage[i % 2], 16 * (i // 2 + 1))
                if 2 <= i < 2 + 2 * E and (i - 2) // 2 >= 2:
                    act.wait_ge(s_blk[(i - 2) // 2 % 2], 16 * ((i - 2) // 4))
                A(chunks[i][1], match(stage(i), chunks[i][1]), ACT.Copy, scale=WSCALE).then_inc(s_hi, 1)
                if i == 3:
                    act.wait_ge(s_const, 16 * len(consts))
                    A(small[:, 256:288], small[:, 0:32], ACT.Exp, scale=-1.0).then_inc(s_ga, 1)
            act.wait_ge(s_set, LOGITS_READY)
            A(route[:, 16:20], route[:, 0:4], ACT.Exp, bias=route[:, 12:13], accum_out=route[:, 13:14]
              ).then_inc(s_ga, 1)
            act.wait_ge(s_set, SETUP_DONE)

            def moe(step, b):
                kind, j, g = step
                blk = wshared[:] if j == 0 else wsel[:, j - 1, :]
                bias = blk[:, 4 * W:].bitcast(F32)
                if kind == "L1":
                    n = 12 * b + 4 * j + g
                    act.wait_ge(s_l1, n + 1)
                    wait(act, s_hs, n - 1)
                    for m in range(2):
                        ins = A(hf[:, g % 2, m * T:(m + 1) * T], l1_bank[g % 2][:, m * T:(m + 1) * T],
                                ACT.Gelu_apprx_tanh, bias=bias[:, 2 * g + m:2 * g + m + 1], scale=UN)
                    ins.then_inc(s_gel, 1)
                elif g == HC // 2 - 1:
                    u = 3 * b + j
                    act.wait_ge(s_l2, u + 1)
                    if j == 0:
                        wait(act, s_cs, b)
                    else:
                        wait(act, s_acc, 2 * b + j - 1)
                    for m in range(KC):
                        ins = A((acc if j == 0 else yb)[:, m, :], y_bank[:, m * T:(m + 1) * T], ACT.Identity,
                                bias=bias[:, HC + m:HC + m + 1], scale=UN)
                    ins.then_inc(s_y, 1)

            def att(step, a):
                kind = step[0]
                if kind == "V":
                    act.wait_ge(s_qkv, 3 * a + 3)
                    wait(act, s_pv, 4 * a)
                    A(vp[:, :, :, 0:HEAD], bC[:].rearrange("p (t h e) -> p t h e", t=TT, h=NH), ACT.Copy
                      ).then_inc(s_v, 1)
                elif kind in ("TK", "TQ"):
                    first = 0 if kind == "TK" else 2 + 2 * step[1]
                    dst = kT if kind == "TK" else qT
                    if kind == "TK" or step[1] == 0:
                        wait(act, s_st, 8 * a)
                    else:
                        act.wait_ge(s_sn, 16 * a + 16)
                    for half in range(2):
                        act.wait_ge(s_tr, 6 * a + first + half + 1)
                        bank = ((bD, bE) if kind == "TK" else (bA, bB))[half]
                        A(dst[:, 4 * half:4 * half + 4, :], bank[:].bitcast(F16).rearrange("p (g t) -> p g t", g=4),
                          ACT.Copy).then_inc(s_te, 1)
                elif kind == "ST":
                    pair = step[1]
                    act.wait_ge(s_st, 8 * a + pair + 1)
                    quad = pair // 2
                    wait(act, s_pv, 4 * a + max(quad - 1, 0))
                    for n in range(2):
                        bank = ((bA, bB), (bC, bD))[pair % 2][n]
                        ins = A(probs[:, quad % 2, 2 * (pair % 2) + n, :, :],
                                bank[:].rearrange("p (k q) -> p k q", k=KC), ACT.Exp)
                    ins.then_inc(s_exp, 1)
                elif kind == "PV" and step[1] % 2 == 1:
                    q = step[1] // 2
                    act.wait_ge(s_pv, 4 * a + step[1] + 1)
                    wait(act, s_on, 2 * a)
                    A(oT[:, 2 * q:2 * q + 2, :], bE[:].rearrange("p (n q) -> p n q", n=2), ACT.Copy
                      ).then_inc(s_oe, 1)
                elif kind == "AT":
                    act.wait_ge(s_at, a + 1)
                    wait(act, s_pp, a)
                    A(aT[:], bC[:].bitcast(F16).rearrange("p (n c t) -> p n c t", n=2, c=KC), ACT.Copy
                      ).then_inc(s_ate, 1)
                elif kind == "PJ":
                    act.wait_ge(s_pp, a + 1)
                    wait(act, s_x2, a)
                    for m in range(KC):
                        ins = A(xo[:, m, :], bD[:, m * T:(m + 1) * T], ACT.Identity, bias=pbias[:, m:m + 1], scale=UN)
                    ins.then_inc(s_pj, 1)

            def emit(steps, b, a):
                for step in steps:
                    if step[0] in ("L1", "L2"):
                        moe(step, b)
                    else:
                        att(step, a)

            phases(act, emit)

            def lstm_body(i):
                for s in range(BODY):
                    t = BODY * i + s
                    ifg, o = ifg_bank[s // SB], o_bank[s // SB]
                    act.wait_ge(s_if, t + 1)
                    wait(act, s_pr, t)
                    A(sif[:], ifg[:, 0:4, s % SB, :], ACT.Sigmoid, scale=UN)
                    A(gcell[:, 0:2, :], ifg[:, 4:6, s % SB, :], ACT.Tanh, scale=UN).then_inc(s_sig, 1)
                    act.wait_ge(s_o, t + 1)
                    wait(act, s_hfull, t)
                    A(so[:], o[:, 0:2, s % SB, :], ACT.Sigmoid, scale=UN).then_inc(s_o_used, 1)
                    act.wait_ge(s_c, t + 1)
                    A(tc_[:], gcell[:, 2:4, :], ACT.Tanh).then_inc(s_tc, 1)

            lstm_body(0)
            with act.Fori(1, T // BODY) as i:
                lstm_body(i)

            def adapter_body(i):
                for n in range(2):
                    b = 2 * i + n
                    act.wait_ge(s_dn, b + 1)
                    wait(act, s_rs, 2 * i)
                    A(rl[:, n, :], banks[n][0:R, 0:T], ACT.Relu, scale=UN,
                      bias=hsel[0:R, n, EB - 2:EB].bitcast(F32)).then_inc(s_rl, 1)
                    act.wait_ge(s_fo, b + 1)
                    wait(act, s_out[n], 16 * i)
                    A(obuf[:, n, :], banks[4 + n][:], ACT.Copy, scale=UN).then_inc(s_ob, 1)

            adapter_body(0)
            with act.Fori(1, B // 2) as i:
                adapter_body(i)

        @block.vector
        def _(dve):
            V = nc.vector
            UN = 1.0 / WSCALE
            chain = [0]

            def link(ins):
                chain[0] += 1
                ins.then_inc(s_set, 1)
                dve.wait_ge(s_set, chain[0])

            dve.wait_ge(s_const, 16 * len(consts))
            link(V.memset(adapt[R:P, :, 2 * KC * R:].bitcast(I32), 0))
            link(V.tensor_copy(ident16[:], ident[:]))
            link(V.tensor_scalar(ident64[:], ident[:], WSCALE, None, ALU.mult))
            for raw, dst in ((t1[0:33, :], brow_q[:, 0:512]), (t2[0:33, 0:256], brow_q[:, 512:768]),
                             (hf[0:33, 0, :], brow_l[:, 0:512]), (hf[0:33, 1, :], brow_l[:, 512:1024])):
                link(V.tensor_scalar(dst, raw, WSCALE, None, ALU.mult))
                link(V.scalar_tensor_tensor(dst[32:33], raw[32:33], WSCALE, dst[32:33], ALU.mult, ALU.subtract))
            link(V.tensor_tensor(iv[:], sg[:], sg[:], ALU.mult))
            link(V.reciprocal(iv[:], iv[:]))
            link(V.tensor_tensor(mi2[:], mu[:], iv[:], ALU.mult))
            link(V.tensor_tensor(mmi[:], mu[:], mi2[:], ALU.mult))
            link(V.tensor_scalar(mi2[:], mi2[:], -2.0, None, ALU.mult))
            link(V.tensor_copy(adapt[0:R, :, EB - 2:EB].bitcast(F32), dbias[:].unsqueeze(2)))

            def cut(i):
                src, hi, lo, _ = chunks[i]
                dve.wait_ge(s_hi, i + 1)
                V.scalar_tensor_tensor(lo, match(stage(i), lo), WSCALE, hi, ALU.mult, ALU.subtract).then_inc(s_lo, 1)

            for i in range(max(NCH, B)):
                if i < NCH:
                    cut(i)
                if i < B:
                    dve.wait_ge(s_gx[i % 2], 16 * (i // 2 + 1))
                    for n, (lo, hi) in enumerate(SEGS):
                        ins = V.tensor_reduce(sums[:, n, :, i:i + 1], (xt, xr)[i % 2][:, :, lo:hi], AX.X, ALU.add)
                    ins.then_inc(s_gsum, 1)
            dve.wait_ge(s_gsum, B)
            dve.wait_ge(s_ga, 1)
            link(V.tensor_scalar(small[:, 256:288], small[:, 256:288], 1.0, None, ALU.add))
            link(V.reciprocal(small[:, 256:288], small[:, 256:288]))
            link(V.tensor_tensor(small[:, 32:64], small[:, 0:32], small[:, 256:288], ALU.mult))
            hp, wp = T - LH, T - LH
            link(V.tensor_tensor(agg[:, 2:4], sums[:, 0], sums[:, 2], ALU.add))
            link(V.tensor_tensor(agg[:, 4:6], sums[:, 1], sums[:, 2], ALU.add))
            link(V.tensor_tensor(agg[:, 0:2], agg[:, 2:4], sums[:, 1], ALU.add))
            link(V.tensor_scalar(agg[:, 0:2], agg[:, 0:2], 1.0 / T, None, ALU.mult))
            link(V.tensor_scalar(agg[:, 2:6], agg[:, 2:6], 1.0 / hp, None, ALU.mult))
            assert chain[0] == GATE_READY, chain[0]
            lg, md, mx = route[:, 0:4], route[:, 4:12], route[:, 12:13]
            dve.wait_ge(s_gp, 1)
            link(V.tensor_tensor(lg, bA[0:B, 0:E], grow[:, 0:4], ALU.add))
            link(V.tensor_tensor(md, bB[0:B, 0:2 * E], grow[:, 4:12], ALU.add))
            link(V.scalar_tensor_tensor(lg, md[:, 0:4], 1.0, lg, ALU.add, ALU.mult))
            link(V.tensor_tensor(lg, lg, md[:, 4:8], ALU.add))
            link(V.tensor_reduce(mx, lg, AX.X, ALU.max, negate=True))
            assert chain[0] == LOGITS_READY, chain[0]
            dve.wait_ge(s_ga, 2)
            pr, rc = route[:, 16:20], route[:, 13:14]
            link(V.reciprocal(rc, rc))
            link(V.tensor_scalar(pr, pr, rc, None, ALU.mult))
            one, tmp = (route[:, 32:36], route[:, 36:40]), route[:, 40:44]
            best, pos = (route[:, 44:45], route[:, 45:46]), (route[:, 46:47], route[:, 47:48])
            for n in range(2):
                link(V.tensor_reduce(best[n], pr, AX.X, ALU.max))
                link(V.tensor_scalar(tmp, pr, best[n], None, ALU.is_ge))
                link(V.tensor_tensor(tmp, tmp, rev[:, 4:8], ALU.mult))
                link(V.tensor_reduce(pos[n], tmp, AX.X, ALU.max))
                link(V.tensor_scalar(one[n], rev[:, 4:8], pos[n], None, ALU.is_equal))
                if n == 0:
                    link(V.scalar_tensor_tensor(pr, one[0], -2.0, pr, ALU.mult, ALU.add))
            tot = route[:, 48:49]
            link(V.tensor_tensor(tot, best[0], best[1], ALU.add))
            link(V.tensor_scalar(tot, tot, 1e-8, None, ALU.add))
            link(V.reciprocal(tot, tot))
            row = route[:, 52:60]
            for n in range(2):
                w = row[:, 3 * n + 2:3 * n + 3]
                link(V.tensor_tensor(w, best[n], tot, ALU.mult))
                for s, masked in ((0, 2), (1, 1)):
                    f = row[:, 3 * n + s:3 * n + s + 1]
                    link(V.tensor_scalar(f, one[n][:, masked:masked + 1], -1.0, 1.0, ALU.mult, ALU.add))
                    link(V.tensor_tensor(f, f, w, ALU.mult))
                link(V.tensor_scalar(row[:, 6 + n:7 + n], pos[n], -1.0, float(E), ALU.mult, ALU.add))
            for n in range(8):
                ins = V.tensor_scalar(table[:, :, n], ident[0:B, 0:B], row[:, n:n + 1], None, ALU.mult)
            link(ins)
            assert chain[0] == TABLE_READY, chain[0]
            dve.wait_ge(s_gp, 2)
            link(V.tensor_copy(gates_b[:].rearrange("p b n -> p (b n)"), bC[:, 0:B * 8]))
            V.tensor_copy(idx_moe[:], gates_b[0:1, :, 6:8]).then_inc(s_idx, 1)
            for e in range(EF):
                dve.wait_ge(s_cp, e + 1)
                dve.wait_ge(s_cw, 64 * (e + 1))
                pw = bD[0:R + 1, 0:D]
                hi = adapt[0:R + 1, e, 2 * KC * R:2 * KC * R + D]
                lo = adapt[0:R + 1, e, 2 * KC * R + D:2 * KC * R + 2 * D]
                full = yb[0:R + 1, 0, :]
                link(V.tensor_copy(full, pw))
                link(V.tensor_tensor(cbrow[64:65, :], cbrow[64:65, :], xo[64:65, 0, :], ALU.add))
                link(V.tensor_tensor(yb[64:65, 0, :], yb[64:65, 0, :], cbrow[64:65, :], ALU.add))
                V.tensor_scalar(hi, full, WSCALE, None, ALU.mult).then_inc(s_cd, 1)
                dve.wait_ge(s_cd, 2 * e + 1)
                V.scalar_tensor_tensor(lo, full, WSCALE, hi, ALU.mult, ALU.subtract).then_inc(s_cd, 1)
                dve.wait_ge(s_cd, 2 * e + 2)
            assert chain[0] == SETUP_DONE, chain[0]

            def cut_x(b):
                dve.wait_ge(s_xt, 16 * b + 16)
                wait(dve, s_l1, 12 * b)
                V.tensor_copy(xs[:, 0], xt[:]).then_inc(s_xc, 1)
                dve.wait_ge(s_xc, b + 1)
                V.tensor_tensor(xs[:, 1], xt[:], xs[:, 0], ALU.subtract).then_inc(s_xs, 1)

            def moe(step, b):
                kind, j, g = step
                if kind == "L1":
                    if j == 0 and g == 0:
                        cut_x(b)
                    n = 12 * b + 4 * j + g
                    dve.wait_ge(s_gel, n + 1)
                    wait(dve, s_l2, 3 * b + j)
                    src = hf[:, g % 2, :].rearrange("p (m t) -> p m t", m=2)
                    hi, lo = hh[:, 0, 2 * g:2 * g + 2, :], hh[:, 1, 2 * g:2 * g + 2, :]
                    V.tensor_copy(hi, src).then_inc(s_hh, 1)
                    dve.wait_ge(s_hh, n + 1)
                    V.tensor_tensor(lo, src, hi, ALU.subtract).then_inc(s_hs, 1)
                elif g == HC // 2 - 1:
                    u = 3 * b + j
                    if j >= 1:
                        dve.wait_ge(s_y, u + 1)
                        wait(dve, s_acc, 2 * b + j - 1)
                        for n, (lo, hi) in enumerate(SEGS):
                            w = gates_b[:, bass.ds(b, 1), 3 * (j - 1) + n]
                            ins = V.scalar_tensor_tensor(acc[:, :, lo:hi], yb[:, :, lo:hi], w, acc[:, :, lo:hi],
                                                         ALU.mult, ALU.add)
                        ins.then_inc(s_acc, 1)
                    if j == 2:
                        dve.wait_ge(s_acc, 2 * b + 2)
                        wait(dve, s_qkv, 3 * b)
                        V.tensor_copy(cs[:, 0], acc[:]).then_inc(s_ch, 1)
                        dve.wait_ge(s_ch, b + 1)
                        V.tensor_tensor(cs[:, 1], acc[:], cs[:, 0], ALU.subtract).then_inc(s_cs, 1)

            def att(step, a):
                kind = step[0]
                if kind == "QK":
                    tt = step[1]
                    base = 10 * a + 5 * tt
                    dve.wait_ge(s_qkv, 3 * a + tt + 1)
                    wait(dve, s_qkn, 2 * a + tt)
                    ps = (bA, bB)[tt]
                    psv, t1v, t2v = (x[:].rearrange("p (s h e) -> p s h e", s=2, e=HEAD) for x in (ps, t1, t2))
                    hw = HEAD // 2
                    lo_, hi_ = slice(0, hw), slice(hw, HEAD)

                    def all_heads(table, part, width):
                        return table[:, tt, :, part].unsqueeze(2).to_broadcast([P, 2, NH, width])

                    V.tensor_tensor(t1v, psv, all_heads(cos_t, slice(0, HEAD), HEAD), ALU.mult).then_inc(s_rp, 1)
                    V.tensor_tensor(t2v[:, :, :, lo_], psv[:, :, :, hi_], all_heads(sin_t, lo_, hw), ALU.mult
                                    ).then_inc(s_rp, 1)
                    V.tensor_tensor(t2v[:, :, :, hi_], psv[:, :, :, lo_], all_heads(sin_t, hi_, hw), ALU.mult
                                    ).then_inc(s_rp, 1)
                    dve.wait_ge(s_rp, base + 3)
                    V.tensor_tensor(t1[:], t1[:], t2[:], ALU.add).then_inc(s_rp, 1)
                    dve.wait_ge(s_rp, base + 4)
                    if tt == 0:
                        wait(dve, s_tr, 6 * a)
                    r = t1[:].rearrange("p (h e) -> p h e", e=HEAD)
                    V.tensor_copy(qkn[:, tt, :, 0:16], r).then_inc(s_rp, 1)
                    dve.wait_ge(s_rp, base + 5)
                    V.tensor_tensor(qkn[:, tt, 0:NH, 16:32], r[:, 0:NH], qkn[:, tt, 0:NH, 0:16], ALU.subtract)
                    V.tensor_tensor(qkn[:, tt, NH:, 32:48], r[:, NH:], qkn[:, tt, NH:, 0:16], ALU.subtract
                                    ).then_inc(s_qkn, 1)
                elif kind == "SN":
                    for h in step[1]:
                        dve.wait_ge(s_sn, 16 * a + h + 1)
                        if h == 0:
                            wait(dve, s_mn, a)
                        bank = (bC, bD, bE)[h % 3]
                        V.tensor_reduce(mneg[:, :, h:h + 1], bank[:].rearrange("p (t k) -> p t k", t=TT), AX.X,
                                        ALU.max, negate=True).then_inc(s_mx, 1)
                    if step[1][-1] == NH - 1:
                        dve.wait_ge(s_mx, 16 * a + 16)
                        dve.wait_ge(s_tr, 6 * a + 4)
                        hi, lo = qkn[:, :, 0:NH, KSUM], qkn[:, :, 0:NH, KSUM + 1]
                        V.tensor_copy(hi, mneg[:]).then_inc(s_mh, 1)
                        dve.wait_ge(s_mh, a + 1)
                        V.tensor_tensor(lo, mneg[:], hi, ALU.subtract).then_inc(s_mn, 1)
                elif kind == "ON":
                    for tt in range(TT):
                        dve.wait_ge(s_on, 2 * a + tt + 1)
                        wait(dve, s_an, 2 * a + tt)
                        wait(dve, s_mo, 16 * a)
                        o = (bA, bB)[tt][:].rearrange("p (h e) -> p h e", e=32)
                        V.reciprocal(recs[:, tt, :], o[:, :, HEAD]).then_inc(s_rc, 1)
                        dve.wait_ge(s_rc, 2 * a + tt + 1)
                        V.tensor_tensor(an[:, tt, :].rearrange("p (h e) -> p h e", e=HEAD), o[:, :, 0:HEAD],
                                        recs[:, tt, :].unsqueeze(2).to_broadcast([P, NH, HEAD]), ALU.mult
                                        ).then_inc(s_an, 1)
                    dve.wait_ge(s_mi, 16 * B * (a + 1))
                    wait(dve, s_at, a)
                    V.tensor_copy(ah[:, 0], arow[:]).then_inc(s_ah, 1)
                    dve.wait_ge(s_ah, a + 1)
                    V.tensor_tensor(ah[:, 1], arow[:], ah[:, 0], ALU.subtract).then_inc(s_as, 1)
                elif kind == "PJ":
                    dve.wait_ge(s_pj, a + 1)
                    dve.wait_ge(s_xr, 16 * a + 16)
                    V.tensor_tensor(xo[:], xo[:], xr[:], ALU.add).then_inc(s_xa, 1)
                    dve.wait_ge(s_xa, a + 1)
                    hi, lo = (x[:, :, bass.ds(LT * a, LT), :].rearrange("p c t b -> p c (t b)") for x in (x2h, x2l))
                    V.tensor_copy(hi, xo[:]).then_inc(s_xh, 1)
                    dve.wait_ge(s_xh, a + 1)
                    V.tensor_tensor(lo, xo[:], hi, ALU.subtract).then_inc(s_x2, 1)

            def emit(steps, b, a):
                for step in steps:
                    if step[0] in ("L1", "L2"):
                        moe(step, b)
                    else:
                        att(step, a)

            phases(dve, emit)

            h0 = condt
            dve.wait_ge(s_l2, 3 * B)
            V.memset(gcell[:], 0.0)
            V.memset(stat[:], 0.0).then_inc(s_h0, 1)
            dve.wait_ge(s_h0, 1)
            V.tensor_copy(hs_hi[:, BODY - 1], h0).then_inc(s_h, 1)
            dve.wait_ge(s_h, 1)
            V.tensor_tensor(hs_lo[:, BODY - 1], h0, hs_hi[:, BODY - 1], ALU.subtract).then_inc(s_hl, 1)

            def lstm_body(i):
                for s in range(BODY):
                    t = BODY * i + s
                    dve.wait_ge(s_sig, t + 1)
                    wait(dve, s_c, t)
                    V.tensor_tensor(prod[:], sif[:], gcell[:], ALU.mult).then_inc(s_pr, 1)
                    dve.wait_ge(s_pr, t + 1)
                    wait(dve, s_tc, t)
                    V.tensor_tensor(gcell[:, 2:4], prod[:, 0:2], prod[:, 2:4], ALU.add).then_inc(s_c, 1)
                    dve.wait_ge(s_tc, t + 1)
                    dve.wait_ge(s_o_used, t + 1)
                    if s == 0:
                        wait(dve, s_hist, i)
                    V.tensor_tensor(hs_hi[:, s], so[:], tc_[:], ALU.mult).then_inc(s_h, 1)
                    V.tensor_tensor(hs_f[:, s], so[:], tc_[:], ALU.mult).then_inc(s_hfull, 1)
                    dve.wait_ge(s_hfull, t + 1)
                    V.tensor_tensor(hs_lo[:, s], hs_f[:, s], hs_hi[:, s], ALU.subtract).then_inc(s_hl, 1)
                by_t = lambda x: x[:].rearrange("p t c b -> p (c b) t")
                V.tensor_tensor(hsq[:], hs_f[:], hs_f[:], ALU.mult).then_inc(s_stat, 1)
                V.tensor_reduce(stat[:, 0, :], by_t(hs_f), AX.X, ALU.add).then_inc(s_stat, 1)
                dve.wait_ge(s_stat, 4 * i + 2)
                V.tensor_reduce(stat[:, 1, :], by_t(hsq), AX.X, ALU.add).then_inc(s_stat, 1)
                dve.wait_ge(s_stat, 4 * i + 3)
                V.tensor_tensor(stat[:, 2:4, :], stat[:, 2:4, :], stat[:, 0:2, :], ALU.add).then_inc(s_stat, 1)
                dve.wait_ge(s_stat, 4 * i + 4)

            lstm_body(0)
            with dve.Fori(1, T // BODY) as i:
                lstm_body(i)

            fchain = [0]

            def flink(ins):
                fchain[0] += 1
                ins.then_inc(s_fd, 1)
                dve.wait_ge(s_fd, fchain[0])

            V.memset(rs_[R:R + 1, :, 0, :], 1.0)
            V.memset(rs_[R:R + 1, :, 1, :], 0.0)
            flink(V.tensor_scalar(stat[:, 2:4, :], stat[:, 2:4, :], 1.0 / T, None, ALU.mult))
            assert fchain[0] == STATS_READY
            dve.wait_ge(s_fl, 1)
            ls, tf = route[:, 0:8], route[:, 8:16]
            flink(V.tensor_scalar(ls, bA[0:B, 0:EF], -1.0 / D, None, ALU.mult))
            flink(V.tensor_reduce(route[:, 25:26], ls, AX.X, ALU.max))
            flink(V.tensor_scalar(tf, ls, route[:, 25:26], None, ALU.is_ge))
            flink(V.tensor_tensor(tf, tf, rev[:], ALU.mult))
            flink(V.tensor_reduce(route[:, 26:27], tf, AX.X, ALU.max))
            flink(V.tensor_scalar(route[:, 24:25], route[:, 26:27], -1.0, float(EF), ALU.mult, ALU.add))
            assert fchain[0] == INDEX_READY
            dve.wait_ge(s_fl, 2)
            flink(V.tensor_copy(idx_ffn[:], bB[0:1, 0:B]))

            def adapter_body(i):
                for n in range(2):
                    b = 2 * i + n
                    wait(dve, s_fo, 2 * i)
                    e = dve.value_load(idx_ffn[0:1, bass.ds(b, 1)], min_val=0, max_val=EF - 1)
                    V.tensor_copy(hsel[:, n, :].bitcast(I32).unsqueeze(1), adapt[:].bitcast(I32)[:, bass.ds(e, 1), :]
                                  ).then_inc(s_sel, 1)
                for n in range(2):
                    b = 2 * i + n
                    dve.wait_ge(s_rl, b + 1)
                    V.tensor_copy(rs_[0:R, n, 0, :], rl[:, n, :]).then_inc(s_rh, 1)
                    dve.wait_ge(s_rh, b + 1)
                    V.tensor_tensor(rs_[0:R, n, 1, :], rl[:, n, :], rs_[0:R, n, 0, :], ALU.subtract
                                    ).then_inc(s_rs, 1)

            adapter_body(0)
            with dve.Fori(1, B // 2) as i:
                adapter_body(i)


def kernel(**inputs):
    import numpy as np
    import concourse.bacc as _bacc
    from concourse import mybir as _mybir
    from concourse.bass_utils import run_bass_kernel_spmd as _run

    v = {k: np.asarray(a) for k, a in inputs.items()}
    con = np.ascontiguousarray

    def cols(a, c):
        return con(a.reshape((c, P) + a.shape[1:]).swapaxes(0, 1))

    pos = np.arange(256, dtype=np.float32)
    inv = (1.0 / 10000.0 ** (np.arange(0, HEAD, 2, dtype=np.float32) / np.float32(HEAD))).astype(np.float32)
    ang = (pos[:, None] * inv[None, :]).astype(np.float32)
    cos = np.concatenate([np.cos(ang), np.cos(ang)], -1).astype(np.float32)
    sin = np.concatenate([-np.sin(ang), np.sin(ang)], -1).astype(np.float32)
    scale_q, scale_k = np.float32(HEAD ** -0.5 / WSCALE), np.float32(1.0 / WSCALE)

    def rotary(t):
        return cols(np.stack([t * scale_q, t * scale_k], 1), 2)

    eb = np.concatenate([v["L0_cond_eb1"].reshape(4, 8, P).swapaxes(1, 2),
                         v["L0_cond_eb2"].reshape(4, 2, P).swapaxes(1, 2)], 2)
    sbias = np.concatenate([v["L0_cond_sb1"].reshape(8, P).T, v["L0_cond_sb2"].reshape(2, P).T], 1)
    up = np.concatenate([v["L0_ffn_up_W"].transpose(0, 2, 1), v["L0_ffn_up_b"][:, :, None]], 2)
    arrays = {
        "xT": v["x"].transpose(0, 2, 1).reshape(16, 2, P, 256).transpose(0, 2, 1, 3),
        "xL": v["x"].reshape(16, 16, 16, 2, P).transpose(1, 4, 3, 2, 0).reshape(16, P, 2, 256),
        "condT": cols(v["cond_1024"].T, 2),
        "gw": cols(v["L0_cond_gate_w"], 6), "tw": cols(v["L0_cond_time_w"], 2),
        "grow": np.concatenate([v["L0_cond_gate_b"], v["L0_cond_time_b"]]),
        "ew1": v["L0_cond_ew1"], "ew2": v["L0_cond_ew2"], "sw1": v["L0_cond_sw1"], "sw2": v["L0_cond_sw2"],
        "ebias": eb, "sbias": sbias,
        "qkvT": v["L0_attn_qkv_w"].T, "qb": v["L0_attn_qkv_b"][None], "projT": v["L0_attn_proj_w"].T,
        "pbias": v["L0_attn_proj_b"].reshape(2, P).T,
        "wx": v["L0_cond2_Wx"], "wh": v["L0_cond2_Wh"], "lb": v["L0_cond2_b"][None],
        "baseT": v["L0_ffn_base_W"].T, "bb": v["L0_ffn_base_b"][None],
        "muT": cols(v["L0_ffn_disc_mu"].T, 2), "sgT": cols(v["L0_ffn_disc_sigma"].T, 2),
        "downT": v["L0_ffn_down_W"].reshape(8, 2, P, 64).transpose(2, 0, 1, 3).reshape(P, 8, 128),
        "downbT": v["L0_ffn_down_b"].T,
        "upT": up.reshape(8, 2, P, 65).swapaxes(1, 2),
        "convT": v["L0_ffn_conv_W"].transpose(0, 2, 1).reshape(8, 2, P, 256).swapaxes(1, 2),
        "cb": v["L0_ffn_conv_b"],
        "ident": np.eye(P, dtype=np.float32), "rev": np.arange(8, 0, -1).astype(np.float32),
        "cos_t": rotary(cos), "sin_t": rotary(sin),
    }
    arrays = {k: con(a) for k, a in arrays.items()}
    nc = _bacc.Bacc("TRN2", target_bir_lowering=False, num_devices=1)
    d = {k: nc.dram_tensor(f"in_{k}", a.shape, _mybir.dt.from_np(a.dtype), kind="ExternalInput").ap()
         for k, a in arrays.items()}
    d["out"] = nc.dram_tensor("out_y", (16, 256, 256), _mybir.dt.float32, kind="ExternalOutput").ap()
    mixer_kernel(nc, d)
    r = _run(nc, [{f"in_{k}": a for k, a in arrays.items()}], core_ids=[0])
    return r.results[0]["out_y"]
```

```python
from contextlib import ExitStack

import concourse.bass as bass
from concourse import mybir

ALU = mybir.AluOpType
ACT = mybir.ActivationFunctionType
AX = mybir.AxisListType
F32 = mybir.dt.float32
F16 = mybir.dt.float16
I32 = mybir.dt.int32

P = 128
GELU_A = 0.7978845608028654 * 0.044715
GELU_C = 1.0 / 0.044715
WSCALE = 64.0
HEAD = 16
SLOT = 64
KSUM = 48
KMAX = 50


GATE_READY, LOGITS_READY, TABLE_READY, SETUP_DONE = 46, 51, 80, 81
STATS_READY, INDEX_READY = 2, 8
ROWS_CLEAR, ALL_FILLED = 2, 12


def match(flat, like):
    return flat if len(like.shape) == 2 else flat.rearrange("p (a n) -> p a n", a=like.shape[1])


def wait(engine, sem, value):
    if not (isinstance(value, int) and value <= 0):
        engine.wait_ge(sem, value)


def mixer_kernel(nc, d):
    B, T, D = 16, 256, 256
    KC = D // P
    TT = T // P
    HID = d["ew1"].shape[2]
    HC = HID // P
    E = d["ew1"].shape[0]
    NH = D // HEAD
    EF = d["convT"].shape[0]
    R = d["upT"].shape[3] - 1
    G4 = 4 * D
    GC = G4 // P
    W = KC * HID
    BIAS = HC + KC
    BLK = 4 * W + 2 * BIAS
    LH = T // 3
    SEGS = [(0, LH), (LH, 2 * LH), (2 * LH, T)]
    GROUPS = HC // 2
    RING = 6
    EB = 2 * KC * R + 2 * D + 2

    LT = T // B
    mixed = nc.dram_tensor("mixed", [T, D], F32, kind="Internal").ap()
    resid = nc.dram_tensor("resid", [T, B, D], F32, kind="Internal").ap()
    adapters = nc.dram_tensor("adapters", [P, EF * EB], F16, kind="Internal").ap()
    scratch = nc.dram_tensor("expert_blocks", [E, P, BLK], F16, kind="Internal").ap()

    with ExitStack() as ctx:
        def sb(name, shape, dt=F32):
            return ctx.enter_context(nc.sbuf_tensor(name, shape, dt))

        def sem(name):
            return ctx.enter_context(nc.semaphore(name))

        banks = [ctx.enter_context(nc.psum_tensor(f"bank{i}", [P, 512], F32)) for i in range(8)]
        l1_bank = banks[0:2]
        y_bank = banks[2]
        bA, bB, bC, bD = banks[3:7]
        h_bank = banks[7]

        wsel = sb("wsel", [P, 2, BLK], F16)
        wshared = sb("wshared", [P, BLK], F16)
        hist = sb("hist", [P, 2, KC, B, T], F16)
        lstm_w = sb("lstm_w", [P, 2, 2, KC * G4], F16)
        base_w = sb("base_w", [P, 2, KC * D], F16)
        qkv_w = sb("qkv_w", [P, 2, KC * 3 * D], F16)
        proj_w = sb("proj_w", [P, 2, KC * D], F16)
        ident = sb("ident", [P, P])
        ident16 = sb("ident16", [P, P], F16)
        ident64 = sb("ident64", [P, P], F16)
        cos_t = sb("cos_t", [P, TT, 2, HEAD])
        sin_t = sb("sin_t", [P, TT, 2, HEAD])
        brow_q = sb("brow_q", [33, 3 * D], F16)
        lbias = sb("lbias", [P, GC])
        ones33 = sb("ones33", [33, P], F16)
        pbias = sb("pbias", [P, KC])
        gates_b = sb("gates_b", [P, B, 8])
        idx_moe = sb("idx_moe", [1, B, 2], I32)
        idx_ffn = sb("idx_ffn", [1, B], I32)

        xt = sb("xt", [P, KC, T])
        xr = sb("xr", [P, KC, T])
        xs = sb("xs", [P, 2, KC, T], F16)
        vb = sb("vb", [P, 2, 2 * T])
        sq = sb("sq", [P, 3, 2 * T])
        hh = sb("hh", [P, 2, HC, T], F16)
        acc = sb("acc", [P, KC, T])
        yb = sb("yb", [P, KC, T])
        cs = sb("cs", [P, 2, KC, T], F16)
        t1 = sb("t1", [P, 2 * D])
        t2 = sb("t2", [P, 2 * D])
        qkn = sb("qkn", [P, TT, 2 * NH, SLOT], F16)
        vp = sb("vp", [P, TT, NH, 32])
        kT = sb("kT", [P, NH // 2, T], F16)
        qT = sb("qT", [P, NH // 2, T], F16)
        probs = sb("probs", [P, RING, KC, T])
        oT = sb("oT", [P, 4, T])
        an = sb("an", [P, TT, D])
        arow = an
        ah = sb("ah", [P, 2, TT, D], F16)
        aT = sb("aT", [P, 2, KC, T], F16)
        x2 = sb("x2", [P, 2, KC, T], F16)
        xw = sb("xw", [P, GC, LT, B])
        hs_f = sb("hs_f", [P, LT, KC, B])
        hs = sb("hs", [P, 2, KC, LT, B], F16)
        pre = sb("pre", [P, GC, B])
        uifo = sb("uifo", [P, 6, B])
        gcell = sb("gcell", [P, 4, B])
        prod = sb("prod", [P, 4, B])
        tanc = sb("tanc", [P, KC, B])
        stat = sb("stat", [P, 4, KC * B])
        rbuf = yb[:].rearrange("p c t -> p (c t)")
        mneg = sb("mneg", [P, TT, NH])
        recs = sb("recs", [P, TT, NH])
        small = sb("small", [P, 448])

        hist_flat = hist[:].rearrange("p n c b t -> p (n c b t)")
        adapt = hist_flat[:, 0:EF * EB].rearrange("p (e n) -> p e n", e=EF)
        raw_w = hist_flat[:, 4 * W:].bitcast(F32)
        def halves(t):
            return t[:, 0, :], t[:, 1, :]

        block = ctx.enter_context(nc.Block())

        whi, wlo = halves(lstm_w[:, 0]), halves(lstm_w[:, 1])
        chunks = []

        def block_parts(t):
            return [(t[:, 0:W], t[:, W:2 * W]), (t[:, 2 * W:3 * W], t[:, 3 * W:4 * W])]

        def rows(ap):
            return ap.rearrange("(c p) n -> p c n", p=P)

        for src, (hi, lo) in zip((d["sw1"], d["sw2"]), block_parts(wshared)):
            chunks.append((rows(src), hi, lo, None, WSCALE))
        for e in range(E):
            for n, (src, (hi, lo)) in enumerate(zip((d["ew1"][e], d["ew2"][e]), block_parts(wsel[:, e % 2, :]))):
                chunks.append((rows(src), hi, lo, e if n == 1 else None, WSCALE))
        chunks.append((rows(d["qkvT"]), qkv_w[:, 0, :], qkv_w[:, 1, :], None, WSCALE))
        chunks.append((rows(d["projT"]), proj_w[:, 0, :], proj_w[:, 1, :], None, WSCALE))
        chunks.append((rows(d["wx"]), whi[0], whi[1], None, WSCALE))
        chunks.append((rows(d["wh"]), wlo[0], wlo[1], None, WSCALE / 2))
        chunks.append((rows(d["baseT"]), base_w[:, 0, :], base_w[:, 1, :], None, WSCALE / 2))
        chunks.append((d["downT"], adapt[:, :, 0:KC * R], adapt[:, :, KC * R:2 * KC * R], None, WSCALE / 2))
        NCH = len(chunks)
        def stage(i):
            src = chunks[i][0]
            n = 1
            for s in src.shape[1:]:
                n *= s
            flat = raw_w[:, (i % 2) * W:(i % 2) * W + n]
            return flat

        def as_3d(flat, src):
            return flat.rearrange("p (c n) -> p c n", c=src.shape[1])

        s_stage = [sem("s_stage0"), sem("s_stage1")]
        s_hi = sem("s_hi")
        s_lo = sem("s_lo")
        s_blk = [sem("s_blk0"), sem("s_blk1")]
        s_bias = sem("s_bias")
        s_const = sem("s_const")
        s_gx = [sem("s_gx0"), sem("s_gx1")]
        s_gsum = sem("s_gsum")
        s_set = sem("s_set")
        s_gp = sem("s_gp")
        s_ga = sem("s_ga")
        s_idx = sem("s_idx")
        s_cw = sem("s_cw")
        s_cp = sem("s_cp")
        s_cd = sem("s_cd")
        s_pool = sem("s_pool")

        condt = small[:, 0:32].rearrange("p (c b) -> p c b", c=KC)
        silu = small[:, 32:64].rearrange("p (c b) -> p c b", c=KC)
        agg = small[:, 64:160].rearrange("p (g b) -> p g b", b=B)
        sums = small[:, 160:256].rearrange("p (s c b) -> p s c b", s=3, c=KC)
        gw = sb("gw", [P, 3 * KC, E])
        tw = sb("tw", [P, KC, 2 * E])
        grow = sb("grow", [16, 12])
        route = sb("route", [16, 160])
        table = sb("table", [16, B, 8])
        ones16 = sb("ones16", [16, P])
        unit = sb("unit", [P, 1], F16)
        mu = sb("mu", [P, KC, EF])
        sg = sb("sg", [P, KC, EF])
        iv = sb("iv", [P, KC, EF])
        mi2 = sb("mi2", [P, KC, EF])
        mmi = sb("mmi", [P, KC, EF])
        onesf = sb("onesf", [P, B])
        rev = sb("rev", [16, 8])
        cbrow = sb("cbrow", [65, D])
        upconv = oT[:].rearrange("p q t -> p (q t)")[:, 0:KC * (R + 1 + D)].rearrange("p (c n) -> p c n", c=KC)
        dbias = sb("dbias", [R, EF])

        consts = [
            (ident[:], d["ident"]), (cos_t[:], d["cos_t"]), (sin_t[:], d["sin_t"]), (pbias[:], d["pbias"]),
            (condt, d["condT"]), (gw[:], d["gw"]), (tw[:], d["tw"]),
            (grow[:], d["grow"].partition_broadcast(16)), (rev[:], d["rev"].partition_broadcast(16)),
            (mu[:], d["muT"]), (sg[:], d["sgT"]), (dbias[:], d["downbT"]),
            (wshared[:, 4 * W:].bitcast(F32), d["sbias"]),
            (t1[0:1, :], d["qb"][:, 0:512]), (t1[32:33, :], d["qb"][:, 0:512]),
            (t2[0:1, 0:256], d["qb"][:, 512:768]), (t2[32:33, 0:256], d["qb"][:, 512:768]),
            (lbias[:], d["lb"]),
        ]

        s_xt = sem("s_xt")
        s_xr = sem("s_xr")
        s_xs = sem("s_xs")
        s_xc = sem("s_xc")
        s_wsel = [sem("s_wsel0"), sem("s_wsel1")]
        s_l1 = sem("s_l1")
        s_vs = sem("s_vs")
        s_z = sem("s_z")
        s_th = sem("s_th")
        s_g2 = sem("s_g2")
        s_hh = sem("s_hh")
        s_hs = sem("s_hs")
        s_l2 = sem("s_l2")
        s_y = sem("s_y")
        s_acc = sem("s_acc")
        s_ch = sem("s_ch")
        s_cs = sem("s_cs")
        s_qkv = sem("s_qkv")
        s_v = sem("s_v")
        s_rp = sem("s_rp")
        s_qkn = sem("s_qkn")
        s_dup = sem("s_dup")
        s_tr = sem("s_tr")
        s_te = sem("s_te")
        s_sn = sem("s_sn")
        s_mx = sem("s_mx")
        s_mh = sem("s_mh")
        s_mn = sem("s_mn")
        s_st = sem("s_st")
        s_exp = sem("s_exp")
        s_pv = sem("s_pv")
        s_oe = sem("s_oe")
        s_on = sem("s_on")
        s_rc = sem("s_rc")
        s_an = sem("s_an")
        s_mo = sem("s_mo")
        s_mi = sem("s_mi")
        s_ah = sem("s_ah")
        s_as = sem("s_as")
        s_at = sem("s_at")
        s_ate = sem("s_ate")
        s_pp = sem("s_pp")
        s_xb = sem("s_xb")
        s_xa = sem("s_xa")
        s_xh = sem("s_xh")
        s_x2 = sem("s_x2")

        RES_SLOT = 3
        LSTM_SLOTS = (8, 9, 10, 11, 12, 13, 15, 16, 17, 18, 20, 21, 23, 0, 1, 2)

        def plan(moe, att, late, res, cut):
            moe_steps = []
            for j in range(3):
                moe_steps += [("L1", j, g) for g in range(GROUPS)]
                moe_steps += [("L2", j, p) for p in range(HC // 2)]
            after = {
                0: [("ON",)], 1: [("QK", 0)], 2: [("QK", 1)], 3: [("V",)], 4: [("TQ", 0), ("AT",)],
                5: [("TK",), ("PJ",)], 6: [("SN", (0, 1)), ("XW", 0), ("XW", 1)],
                7: [("SN", (2, 3)), ("XW", 2), ("XW", 3)], 8: [("SN", (4,))], 9: [("SN", (5,))], 10: [("SN", (6,))],
                11: [("SN", (7,))], 12: [("SN", (8, 9, 10))], 13: [("SN", (11, 12, 13))], 14: [("SN", (14, 15))],
                15: [("TQ", 1)], 16: [("ST", 0)], 17: [("ST", 1)], 18: [("ST", 2), ("PV", 0)], 19: [("ST", 3)],
                20: [("ST", 4), ("PV", 1), ("ST", 5)], 21: [("ST", 6), ("PV", 2)], 22: [("ST", 7)],
                23: [("PV", 3)],
            }
            late_kinds = ("ON", "AT", "PJ", "XW")
            steps = []
            gelu = None
            for n, m in enumerate(moe_steps):
                lag = 3 if n <= RES_SLOT else 2
                lstm = n in LSTM_SLOTS and (res if lag == 3 else late)
                step = (LSTM_SLOTS.index(n), lag) if lstm else None
                steps += [m] if moe else []
                steps += [("LS",) + step] if lstm else []
                steps += [("ZS",) + gelu] if gelu else []
                steps += [("LC",) + step] if lstm else []
                steps += [("TH",) + gelu] if gelu else []
                steps += [("LU",) + step] if lstm else []
                steps += [("LH",) + step] if lstm else []
                steps += [("G2",) + gelu] if gelu else []
                steps += [("AC", m[1])] if moe and m[0] == "L2" and m[2] == HC // 2 - 1 else []
                if res and n == RES_SLOT:
                    steps.append(("RS",))
                steps += [x for x in after.get(n, []) if (late if x[0] in late_kinds else att)]
                if res and n == RES_SLOT + 1:
                    steps.append(("SM",))
                gelu = m[1:] if moe and m[0] == "L1" else None
                if cut and n == 20:
                    steps.append(("CX",))
            return steps

        def phases(engine, emit):
            for b in range(3):
                emit(plan(True, b >= 1, b >= 2, False, True), b)
            with engine.Fori(3, B - 1) as b:
                emit(plan(True, True, True, True, True), b)
            emit(plan(True, True, True, True, False), B - 1)
            for b in range(B, B + 3):
                emit(plan(False, b == B, b <= B + 1, True, False), b)

        adapt_in = wsel[:].rearrange("p j n -> p (j n)")[:, 0:EF * EB].rearrange("p (e n) -> p e n", e=EF)
        tail_space = wshared[:, 0:4 * W].bitcast(F32)
        hsel = wsel[:, 1, 0:2 * EB].rearrange("p (j n) -> p j n", j=2)
        rl = tail_space[0:R, 0:2 * T].rearrange("p (n t) -> p n t", n=2)
        obuf = tail_space[:, 512:1536].rearrange("p (n t) -> p n t", n=2)
        rin = tail_space[:, 1536:3584].rearrange("p (n t) -> p n t", n=4)

        rs_ = t1[0:R + 1, :].bitcast(F16).rearrange("p (n k t) -> p n k t", n=2, k=2)

        s_h0 = sem("s_h0")
        s_xp = sem("s_xp")
        s_xe = sem("s_xe")
        s_hp = sem("s_hp")
        s_pa = sem("s_pa")
        s_pre = sem("s_pre")
        s_sig = sem("s_sig")
        s_pr = sem("s_pr")
        s_c = sem("s_c")
        s_tc = sem("s_tc")
        s_hq = sem("s_hq")
        s_h = sem("s_h")
        s_sm = sem("s_sm")
        s_hist = sem("s_hist")
        s_r = sem("s_r")
        s_re = sem("s_re")
        s_rd = sem("s_rd")
        s_ain = sem("s_ain")
        s_rin = [sem(f"s_rin{n}") for n in range(4)]
        s_fl = sem("s_fl")
        s_fd = sem("s_fd")
        s_fidx = sem("s_fidx")
        s_sel = sem("s_sel")
        s_dn = sem("s_dn")
        s_rl = sem("s_rl")
        s_rh = sem("s_rh")
        s_rs = sem("s_rs")
        s_fo = sem("s_fo")
        s_ob = sem("s_ob")
        s_out = [sem("s_out0"), sem("s_out1")]

        @block.sync
        def _(sp):
            def load_chunk(i):
                src = chunks[i][0]
                sp.dma_start(as_3d(stage(i), src), src).then_inc(s_stage[i % 2], 16)

            load_chunk(0)
            load_chunk(1)
            sp.wait_ge(s_pool, ROWS_CLEAR)
            for dst, src in consts:
                sp.dma_start(dst, src).then_inc(s_const, 16)
            for b in range(2):
                sp.dma_start((xt, xr)[b][:], d["xT"][b]).then_inc(s_gx[b], 16)

            def adapter_load(e):
                if e >= 1:
                    sp.wait_ge(s_cd, 2 * e)
                sp.dma_start(upconv[:, :, 0:R + 1], d["upT"][e]).then_inc(s_cw, 16)
                sp.dma_start(upconv[:, :, R + 1:], d["convT"][e]).then_inc(s_cw, 16)
                sp.dma_start(cbrow[64:65, :], d["cb"][e:e + 1, :]).then_inc(s_cw, 16)
                sp.dma_start(t2[64:65, 0:D], d["bb"]).then_inc(s_cw, 16)

            for i in range(2, NCH):
                sp.wait_ge(s_hi, i - 1)
                sp.wait_ge(s_lo, i - 1)
                load_chunk(i)
                e = chunks[i - 2][3]
                if e is not None:
                    sp.dma_start(scratch[e][:, 0:4 * W], wsel[:, e % 2, 0:4 * W]).then_inc(s_blk[e % 2], 16)
                    sp.dma_start(scratch[e][:, 4 * W:].bitcast(F32), d["ebias"][e]).then_inc(s_bias, 16)
                if i < 2 + EF:
                    adapter_load(i - 2)
                if i < B:
                    sp.wait_ge(s_gsum, i - 1)
                    sp.dma_start((xt, xr)[i % 2][:], d["xT"][i]).then_inc(s_gx[i % 2], 16)
            for b in range(min(NCH, B), B):
                sp.wait_ge(s_gsum, b - 1)
                sp.dma_start((xt, xr)[b % 2][:], d["xT"][b]).then_inc(s_gx[b % 2], 16)
            def x_load(b):
                wait(sp, s_xs, b)
                sp.dma_start(xt[:], d["xT"][bass.ds(b, 1)].rearrange("o p c t -> (o p) c t")).then_inc(s_xt, 16)

            sp.wait_ge(s_gsum, B)
            x_load(0)
            for n in range(2):
                sp.wait_ge(s_blk[n], 16 * E // 2)
            sp.wait_ge(s_bias, 16 * E)
            sp.wait_ge(s_idx, 1)
            sp.wait_ge(s_set, SETUP_DONE)
            sp.wait_ge(s_lo, NCH)
            sp.wait_ge(s_hi, NCH)

            def expert_load(b, j):
                if not (isinstance(b, int) and b == 0):
                    sp.wait_ge(s_y, 3 * b + j - 1)
                e = sp.value_load(idx_moe[0:1, bass.ds(b, 1), j], min_val=0, max_val=E - 1)
                sp.dma_start(wsel[:, j, :].bitcast(I32),
                             scratch.bitcast(I32)[bass.ds(e, 1)].rearrange("o p n -> (o p) n")
                             ).then_inc(s_wsel[j], 16)

            def mix(c):
                sp.wait_ge(s_an, 2 * c + 2)
                sp.dma_start(mixed.rearrange("(t p) n -> p t n", p=P), an[:]).then_inc(s_mo, 16)
                sp.wait_ge(s_mo, 16 * c + 16)
                for tt in range(TT):
                    src = mixed[tt * P:(tt + 1) * P, :].rearrange("(t r) (h e) -> t h r e", r=LT, e=HEAD)
                    for t in range(P // LT):
                        sp.dma_start(arow[t * B:(t + 1) * B, tt, :].rearrange("h (r e) -> h r e", e=HEAD), src[t]
                                     ).then_inc(s_mi, 16)

            def late_x_load(c):
                wait(sp, s_x2, c)
                sp.dma_start(xr[:], d["xL"][bass.ds(c, 1)].rearrange("o p c t -> (o p) c t")).then_inc(s_xr, 16)

            def residual_store(r):
                sp.wait_ge(s_re, r + 1)
                dst = resid[bass.ds(LT * r, LT)].rearrange("(n t) b k -> (t b) n k", n=TT)
                sp.dma_start(dst, rbuf.rearrange("p (n k) -> p n k", n=TT)).then_inc(s_rd, 16)

            def transfers(moe, late, res, b):
                if moe:
                    if not (isinstance(b, int) and b == 0):
                        x_load(b)
                    expert_load(b, 0)
                if late:
                    late_x_load(b - 2)
                    mix(b - 2)
                if moe:
                    expert_load(b, 1)
                if res:
                    residual_store(b - 3)

            transfers(True, False, False, 0)
            sp.wait_ge(s_cd, 2 * EF)
            sp.dma_start(adapters.bitcast(I32), hist_flat[:, 0:EF * EB].bitcast(I32)).then_inc(s_rd, 16)
            sp.wait_ge(s_rd, 16)
            for b in range(1, 3):
                transfers(True, b >= 2, False, b)
            with sp.Fori(3, B) as b:
                transfers(True, True, True, b)
            for b in range(B, B + 3):
                transfers(False, b <= B + 1, True, b)
                if b == B:
                    sp.wait_ge(s_y, 3 * B)
                    sp.dma_start(wsel[:].rearrange("p j n -> p (j n)")[:, 0:EF * EB].bitcast(I32),
                                 adapters.bitcast(I32)).then_inc(s_ain, 16)
            sp.wait_ge(s_rd, 16 * (B + 1))

            def residual_load(b, n):
                src = resid[:, bass.ds(b, 1), :].rearrange("(t p) o k -> p t (o k)", p=P)
                sp.dma_start(rin[:, n, :].rearrange("p (t k) -> p t k", t=TT), src).then_inc(s_rin[n], 16)

            def store(b, n):
                sp.wait_ge(s_ob, b + 1)
                dst = d["out"][bass.ds(b, 1)].rearrange("o (t p) n -> (o p) t n", p=P)
                sp.dma_start(dst, obuf[:, n % 2, :].rearrange("p (t n) -> p t n", t=TT)).then_inc(s_out[n % 2], 16)

            for n in range(4):
                residual_load(n, n)
            with sp.Fori(0, B // 4 - 1) as i:
                for n in range(4):
                    store(4 * i + n, n)
                    residual_load(4 * i + n + 4, n)
            for n in range(4):
                store(B - 4 + n, n)
            for n in range(2):
                sp.wait_ge(s_out[n], 16 * (B // 2))

        @block.gpsimd
        def _(pool):
            cleared = [0]

            def fill(ap, value):
                cleared[0] += 1
                nc.gpsimd.memset(ap, value).then_inc(s_pool, 1)
                pool.wait_ge(s_pool, cleared[0])

            for t in (t1[0:33, :], t2[0:33, :]):
                fill(t, 0.0)
            assert cleared[0] == ROWS_CLEAR
            for t in (ones33, qkn, vp):
                fill(t[:], 0.0)
            fill(ones16[:], 1.0)
            fill(unit[:], 1.0)
            fill(onesf[:], 1.0)
            fill(ones33[0:1, :], 1.0)
            fill(ones33[32:33, :], 1.0)
            fill(vp[:, :, :, HEAD:HEAD + 1], WSCALE)
            fill(qkn[:, :, NH:2 * NH, KSUM:KMAX], 1.0)
            assert cleared[0] == ALL_FILLED

            def copy(out, in_):
                one = unit[:]
                while len(one.shape) < len(in_.shape):
                    one = one.unsqueeze(2)
                return nc.gpsimd.tensor_tensor(out, in_, one.to_broadcast(list(in_.shape)), ALU.mult)

            def cut_x(b):
                pool.wait_ge(s_xt, 16 * b + 16)
                wait(pool, s_l1, 12 * b)
                copy(xs[:, 0], xt[:]).then_inc(s_xc, 1)
                pool.wait_ge(s_xc, b + 1)
                PT(xs[:, 1], xt[:], xs[:, 0], ALU.subtract).then_inc(s_xs, 1)

            PT = nc.gpsimd.tensor_tensor

            def emit(steps, b):
                for step in steps:
                    if step[0] == "QK":
                        a, tt = b - 1, step[1]
                        pool.wait_ge(s_rp, 10 * a + 5 * tt + 5)
                        r = t1[:].rearrange("p (h e) -> p h e", e=HEAD)
                        PT(qkn[:, tt, 0:NH, 16:32], r[:, 0:NH], qkn[:, tt, 0:NH, 0:16], ALU.subtract)
                        PT(qkn[:, tt, NH:, 32:48], r[:, NH:], qkn[:, tt, NH:, 0:16], ALU.subtract).then_inc(s_qkn, 1)
                        copy(qkn[:, tt, 0:NH, 32:48], qkn[:, tt, 0:NH, 0:16])
                        copy(qkn[:, tt, NH:2 * NH, 16:32], qkn[:, tt, NH:2 * NH, 0:16]).then_inc(s_dup, 1)
                    elif step[0] == "G2":
                        _, j, g = step
                        n = 12 * b + 4 * j + g
                        hi, lo = (hh[:, k, 2 * g:2 * g + 2, :] for k in range(2))
                        s2 = sq[:, (4 * j + g) % 3, :].rearrange("p (m t) -> p m t", m=2)
                        pool.wait_ge(s_g2, n + 1)
                        wait(pool, s_l2, 3 * b + j)
                        copy(hi, s2).then_inc(s_hh, 1)
                        pool.wait_ge(s_hh, n + 1)
                        PT(lo, s2, hi, ALU.subtract).then_inc(s_hs, 1)
                    elif step[0] == "CX":
                        cut_x(b + 1)
                    elif step[0] == "SM":
                        c = b - 3
                        pool.wait_ge(s_h, LT * c + LT + 1)
                        for n in range(2):
                            cp = copy(hist[:, n, :, :, bass.ds(LT * c, LT)],
                                      hs[:, n].rearrange("p c t b -> p c b t"))
                        cp.then_inc(s_hist, 1)

            pool.wait_ge(s_gsum, B)
            cut_x(0)
            phases(pool, emit)

        @block.tensor
        def _(pe):
            mm = nc.tensor.matmul

            for e in range(EF):
                pe.wait_ge(s_cw, 64 * (e + 1))
                if e >= 1:
                    pe.wait_ge(s_cd, 2 * e)
                for c in range(KC):
                    m = mm(bD[0:R + 1, 0:D], upconv[:, c, 0:R + 1], upconv[:, c, R + 1:], start=(c == 0),
                           stop=(c == KC - 1))
                m.then_inc(s_cp, 1)
            pe.wait_ge(s_pool, ALL_FILLED)
            pe.wait_ge(s_const, 16 * len(consts))
            pe.wait_ge(s_set, GATE_READY)
            for g in range(3 * KC):
                mm(bA[0:B, 0:E], agg[:, g, :], gw[:, g, :], start=(g == 0), stop=(g == 3 * KC - 1))
            for c in range(KC):
                m = mm(bB[0:B, 0:2 * E], silu[:, c, :], tw[:, c, :], start=(c == 0), stop=(c == KC - 1))
            m.then_inc(s_gp, 1)
            pe.wait_ge(s_set, TABLE_READY)
            mm(bC[:, 0:B * 8], ones16[:], table[:].rearrange("p b n -> p (b n)"), start=True, stop=True
               ).then_inc(s_gp, 1)
            pe.wait_ge(s_hi, NCH)
            pe.wait_ge(s_lo, NCH)
            pe.wait_ge(s_set, SETUP_DONE)
            pe.wait_ge(s_pool, ALL_FILLED)

            def late(b):
                return not (isinstance(b, int) and b < 2)

            THREE = ((0, 0), (1, 0), (0, 1))

            def moe(step, b):
                _, j, g = step
                blk = wshared[:] if j == 0 else wsel[:, j - 1, :]
                w1 = [blk[:, n * W:(n + 1) * W].rearrange("p (c n) -> p c n", c=KC) for n in range(2)]
                w2 = [blk[:, (2 + n) * W:(3 + n) * W].rearrange("p (c n) -> p c n", c=HC) for n in range(2)]
                if step[0] == "L1":
                    n = 12 * b + 4 * j + g
                    if j == 0 and g == 0:
                        pe.wait_ge(s_xs, b + 1)
                    if j >= 1 and g == 0:
                        pe.wait_ge(s_wsel[j - 1], 16 * b + 16)
                    wait(pe, s_vs, n - 1)
                    if j == 1 and g == 0 and late(b):
                        pe.wait_ge(s_xe, 4 * (b - 2) + 4)
                    bank = l1_bank[g % 2]
                    for m in range(2):
                        ch = 2 * g + m
                        for k, (wp, xp) in enumerate(THREE):
                            for c in range(KC):
                                ins = mm(bank[:, m * T:(m + 1) * T], w1[wp][:, c, ch * P:(ch + 1) * P],
                                         xs[:, xp, c, :], start=(m == 0 and k == 0 and c == 0),
                                         stop=(k == 2 and c == KC - 1), skip_group_check=True)
                    ins.then_inc(s_l1, 1)
                else:
                    u = 3 * b + j
                    if g == 0:
                        wait(pe, s_y, u)
                        if j == 0 and not (isinstance(b, int) and b < 3):
                            pe.wait_ge(s_re, b - 2)
                    pe.wait_ge(s_hs, 4 * u + g + 1)
                    for ch in (2 * g, 2 * g + 1):
                        for k, (wp, hp) in enumerate(THREE):
                            for m in range(KC):
                                ins = mm(y_bank[:, m * T:(m + 1) * T], w2[wp][:, ch, m * P:(m + 1) * P],
                                         hh[:, hp, ch, :], start=(ch == 0 and k == 0 and m == 0),
                                         stop=(ch == HC - 1 and k == 2), skip_group_check=True)
                    if g == HC // 2 - 1:
                        ins.then_inc(s_l2, 1)

            def qk_or_v(a, tt, cols, bank, off, n, start):
                for k, (wp, cp) in enumerate(THREE):
                    for c in range(KC):
                        w = qkv_w[:, wp, :].rearrange("p (c n) -> p c n", c=KC)[:, c, cols:cols + n]
                        mm(bank[:, off:off + n], cs[:, cp, c, tt * P:(tt + 1) * P], w,
                           start=(start and k == 0 and c == 0), stop=False, skip_group_check=True)
                return mm(bank[:, off:off + n], ones33[:, :], brow_q[:, cols:cols + n], start=False, stop=True,
                          skip_group_check=True)

            def head_rows(h, k):
                lo = SLOT * (h % 2)
                return slice(lo, lo + k)

            def att(step, a):
                kind = step[0]
                if kind == "QK":
                    tt = step[1]
                    if tt == 0:
                        pe.wait_ge(s_cs, a + 1)
                        wait(pe, s_an, 2 * a)
                    qk_or_v(a, tt, 0, (bA, bB)[tt], 0, 2 * D, True).then_inc(s_qkv, 1)
                elif kind == "V":
                    pe.wait_ge(s_qkv, 3 * a + 2)
                    wait(pe, s_exp, 16 * a)
                    for tt in range(TT):
                        ins = qk_or_v(a, tt, 2 * D, bC, tt * D, D, tt == 0)
                    ins.then_inc(s_qkv, 1)
                elif kind == "TK" or kind == "TQ":
                    is_k = kind == "TK"
                    if is_k:
                        pe.wait_ge(s_qkn, 2 * a + 2)
                        pe.wait_ge(s_dup, 2 * a + 2)
                        pe.wait_ge(s_v, a + 1)
                        pe.wait_ge(s_te, 6 * a + 1)
                    elif step[1] == 1:
                        pe.wait_ge(s_mn, a + 1)
                        pe.wait_ge(s_te, 6 * a + 4)
                    else:
                        pe.wait_ge(s_qkn, 2 * a + 2)
                        pe.wait_ge(s_dup, 2 * a + 2)
                    for half in range(2):
                        bank = ((bC, bA) if is_k else (bA, bB))[half]
                        out = bank[:].bitcast(F16).rearrange("p (g t) -> p g t", g=4)
                        for g in range(4):
                            h0 = (NH if is_k else 0) + 2 * (4 * half + g)
                            for tt in range(TT):
                                ins = nc.tensor.transpose(out[:, g, tt * P:(tt + 1) * P],
                                                          qkn[:, tt, h0:h0 + 2, :].rearrange("p h s -> p (h s)"),
                                                          ident16[:])
                        ins.then_inc(s_tr, 1)
                elif kind == "SN":
                    for h in step[1]:
                        if h == 0:
                            pe.wait_ge(s_te, 6 * a + 4)
                        if h >= 3:
                            pe.wait_ge(s_mx, 16 * a + h - 2)
                        bank = (bA, bB, bC)[h % 3]
                        r = head_rows(h, KSUM)
                        for tt in range(TT):
                            ins = mm(bank[:, tt * T:(tt + 1) * T], qT[r, h // 2, tt * P:(tt + 1) * P],
                                     kT[r, h // 2, :], start=(tt == 0), stop=True, skip_group_check=True)
                        ins.then_inc(s_sn, 1)
                elif kind == "ST":
                    pair = step[1]
                    if pair == 0:
                        pe.wait_ge(s_te, 6 * a + 6)
                    for n in range(2):
                        h = 2 * pair + n
                        bank = (bA, bB, bC)[h % 3]
                        if h >= 3:
                            pe.wait_ge(s_exp, 16 * a + h - 2)
                        r = head_rows(h, KMAX)
                        for k in range(TT):
                            ins = mm(bank[:, k * T:(k + 1) * T], kT[r, h // 2, k * P:(k + 1) * P],
                                     qT[r, h // 2, :], start=(k == 0), stop=True, skip_group_check=True)
                        ins.then_inc(s_st, 1)
                elif kind == "PV":
                    q = step[1]
                    pe.wait_ge(s_exp, 16 * a + 4 * q + 4)
                    if q == 0:
                        wait(pe, s_x2, a)
                    if q >= 2:
                        pe.wait_ge(s_oe, 2 * a + 1)
                    for k in range(TT):
                        for j in range(4):
                            ins = mm(bD[32 * j:32 * j + 32, (q % 2) * T:(q % 2 + 1) * T], vp[:, k, 4 * q + j, :],
                                     probs[:, (4 * q + j) % RING, k, :], start=(k == 0), stop=(k == TT - 1),
                                     skip_group_check=True)
                    ins.then_inc(s_pv, 1)
                elif kind == "ON":
                    pe.wait_ge(s_oe, 2 * a + 2)
                    pe.wait_ge(s_exp, 16 * a + 16)
                    for tt in range(TT):
                        for q in range(4):
                            ins = nc.tensor.transpose((bA, bB)[tt][:, q * P:(q + 1) * P],
                                                      oT[:, q, tt * P:(tt + 1) * P], ident[:])
                        ins.then_inc(s_on, 1)
                elif kind == "AT":
                    pe.wait_ge(s_as, a + 1)
                    out = bD[:].bitcast(F16).rearrange("p (n c t) -> p n c t", n=2, c=KC)
                    for n in range(2):
                        for c in range(KC):
                            for tt in range(TT):
                                ins = nc.tensor.transpose(out[:, n, c, tt * P:(tt + 1) * P],
                                                          ah[:, n, tt, c * P:(c + 1) * P], ident16[:])
                    ins.then_inc(s_at, 1)
                elif kind == "PJ":
                    pe.wait_ge(s_ate, a + 1)
                    for m in range(KC):
                        for k, (wp, ap) in enumerate(THREE):
                            for c in range(KC):
                                w = proj_w[:, wp, :].rearrange("p (c n) -> p c n", c=KC)[:, c, m * P:(m + 1) * P]
                                ins = mm(bD[:, m * T:(m + 1) * T], w, aT[:, ap, c, :],
                                         start=(m == 0 and k == 0 and c == 0), stop=(k == 2 and c == KC - 1),
                                         skip_group_check=True)
                    ins.then_inc(s_pp, 1)

            wl = [[lstm_w[:, s, n, :].rearrange("p (c n) -> p c n", c=KC) for n in range(2)] for s in range(2)]
            bw = [base_w[:, k, :].rearrange("p (c n) -> p c n", c=KC) for k in range(2)]
            hb = h_bank[:, 0:GC * 2 * B].rearrange("p (g n) -> p g n", g=GC)

            def lstm(step, b):
                kind = step[0]
                if kind == "XW":
                    c, k = b - 2, step[1]
                    if k == 0:
                        pe.wait_ge(s_x2, c + 1)
                        if not (isinstance(b, int) and b >= B):
                            pe.wait_ge(s_vs, 12 * b + 4)
                        else:
                            pe.wait_ge(s_vs, 12 * B)
                    if k >= 2:
                        pe.wait_ge(s_xe, 4 * c + k - 1)
                    elif k < 2:
                        wait(pe, s_xe, 4 * c)
                    bank = l1_bank[k % 2]
                    for m in range(2):
                        g = 2 * k + m
                        for n, (wp, xp) in enumerate(THREE):
                            for cc in range(KC):
                                ins = mm(bank[:, m * T:(m + 1) * T], wl[0][wp][:, cc, g * P:(g + 1) * P],
                                         x2[:, xp, cc, :], start=(m == 0 and n == 0 and cc == 0),
                                         stop=(n == 2 and cc == KC - 1), skip_group_check=True)
                    ins.then_inc(s_xp, 1)
                elif kind == "LS":
                    t = LT * (b - step[2]) + step[1]
                    prev = (step[1] - 1) % LT
                    pe.wait_ge(s_h, t + 1)
                    for g in range(GC):
                        for wp in range(2):
                            for cc in range(KC):
                                ins = mm(hb[:, g, :].rearrange("p (n b) -> p n b", n=2), wl[1][wp][:, cc, g * P:(g + 1) * P],
                                         hs[:, :, cc, prev, :],
                                         start=(g == 0 and wp == 0 and cc == 0), stop=(wp == 1 and cc == 1),
                                         skip_group_check=True)
                    ins.then_inc(s_hp, 1)
                elif kind == "RS":
                    r = b - 3
                    if not (isinstance(b, int) and b >= B):
                        pe.wait_ge(s_y, 3 * b)
                    else:
                        pe.wait_ge(s_y, 3 * B)
                    pe.wait_ge(s_h, LT * r + LT + 1)
                    for tt in range(TT):
                        t0, t1_ = tt * (LT // 2), (tt + 1) * (LT // 2)
                        cols = slice(tt * D, (tt + 1) * D)
                        first = tt == 0
                        for wp, hp in THREE:
                            for cc in range(KC):
                                mm(y_bank[:, cols], hs[:, hp, cc, t0:t1_, :].rearrange("p t b -> p (t b)"), bw[wp][:, cc, :], start=first,
                                   stop=False, skip_group_check=True)
                                first = False
                        for hp in range(2):
                            for cc in range(KC):
                                ins = mm(y_bank[:, tt * D + cc * P:tt * D + (cc + 1) * P],
                                         x2[:, hp, cc, tt * P:(tt + 1) * P], ident64[:], start=False,
                                         stop=(hp == 1), skip_group_check=True)
                    ins.then_inc(s_r, 1)

            def emit(steps, b):
                for step in steps:
                    if step[0] in ("L1", "L2"):
                        moe(step, b)
                    elif step[0] in ("XW", "LS", "RS"):
                        lstm(step, b)
                    elif step[0] in ("ON", "AT", "PJ"):
                        att(step, b - 2)
                    else:
                        att(step, b - 1)

            phases(pe, emit)

            pe.wait_ge(s_fd, STATS_READY)
            k = 0
            st = stat[:].rearrange("p n (c b) -> p n c b", c=KC)
            for lhs, rhs in ((st[:, 3], iv), (st[:, 2], mi2), (None, mmi)):
                for c in range(KC):
                    ins = mm(bA[0:B, 0:EF], onesf[:] if lhs is None else lhs[:, c, :], rhs[:, c, :],
                             start=(k == 0), stop=(k == 5))
                    k += 1
            ins.then_inc(s_fl, 1)
            pe.wait_ge(s_fd, INDEX_READY)
            mm(bB[0:1, 0:B], route[:, 24:25], ident[0:B, 0:B], start=True, stop=True).then_inc(s_fl, 1)

            def adapter_body(i):
                parts = range(2)
                wait(pe, s_ob, 2 * i)
                for n in parts:
                    down = [hsel[:, n, k * KC * R:(k + 1) * KC * R].rearrange("p (c r) -> p c r", c=KC)
                            for k in range(2)]
                    pe.wait_ge(s_sel, 2 * i + n + 1)
                    for k, (wp, hp) in enumerate(THREE):
                        for c in range(KC):
                            rhs = hist[:, hp, c, bass.ds(2 * i + n, 1), :].rearrange("p o t -> p (o t)")
                            ins = mm(banks[n][0:R, 0:T], down[wp][:, c, :], rhs, start=(k == 0 and c == 0),
                                     stop=(k == 2 and c == KC - 1), skip_group_check=True)
                    ins.then_inc(s_dn, 1)
                for n in parts:
                    fold = [hsel[0:R + 1, n, 2 * KC * R + k * D:2 * KC * R + (k + 1) * D] for k in range(2)]
                    pe.wait_ge(s_rs, 2 * i + n + 1)
                    for tt in range(TT):
                        for k, (wp, hp) in enumerate(THREE):
                            ins = mm(banks[4 + n][:, tt * D:(tt + 1) * D], rs_[:, n, hp, tt * P:(tt + 1) * P],
                                     fold[wp], start=(tt == 0 and k == 0), stop=(k == 2), skip_group_check=True)
                    ins.then_inc(s_fo, 1)

            pe.wait_ge(s_hist, B)
            adapter_body(0)
            with pe.Fori(1, B // 2) as i:
                adapter_body(i)

        @block.scalar
        def _(act):
            A = nc.scalar.activation
            UN = 1.0 / WSCALE
            for i in range(NCH):
                _, hi, _, _, scale = chunks[i]
                act.wait_ge(s_stage[i % 2], 16 * (i // 2 + 1))
                if 2 <= i < 2 + 2 * E and (i - 2) // 2 >= 2:
                    act.wait_ge(s_blk[(i - 2) // 2 % 2], 16 * ((i - 2) // 4))
                A(hi, match(stage(i), hi), ACT.Copy, scale=scale).then_inc(s_hi, 1)
                if i == 3:
                    act.wait_ge(s_const, 16 * len(consts))
                    A(small[:, 256:288], small[:, 0:32], ACT.Exp, scale=-1.0).then_inc(s_ga, 1)
            act.wait_ge(s_set, LOGITS_READY)
            A(route[:, 16:20], route[:, 0:4], ACT.Exp, bias=route[:, 12:13], accum_out=route[:, 13:14]
              ).then_inc(s_ga, 1)
            act.wait_ge(s_set, SETUP_DONE)

            def moe(step, b):
                kind, j, g = step
                blk = wshared[:] if j == 0 else wsel[:, j - 1, :]
                bias = blk[:, 4 * W:].bitcast(F32)
                n = 12 * b + 4 * j + g
                if kind == "L1":
                    act.wait_ge(s_l1, n + 1)
                    wait(act, s_g2, n - 1)
                    wait(act, s_hs, n - 2)
                    for m in range(2):
                        for dst, func in ((vb[:, g % 2], ACT.Identity), (sq[:, (4 * j + g) % 3], ACT.Square)):
                            ins = A(dst[:, m * T:(m + 1) * T], l1_bank[g % 2][:, m * T:(m + 1) * T], func,
                                    bias=bias[:, 2 * g + m:2 * g + m + 1], scale=UN)
                    ins.then_inc(s_vs, 1)
                elif kind == "TH":
                    act.wait_ge(s_z, n + 1)
                    s2 = sq[:, (4 * j + g) % 3, :]
                    A(s2, s2, ACT.Tanh, scale=GELU_A).then_inc(s_th, 1)
                elif g == HC // 2 - 1:
                    u = 3 * b + j
                    act.wait_ge(s_l2, u + 1)
                    if j == 0:
                        wait(act, s_cs, b)
                    else:
                        wait(act, s_acc, 2 * b + j - 1)
                        if not (isinstance(b, int) and b < 3):
                            act.wait_ge(s_rd, 16 * (b - 1))
                    for m in range(KC):
                        ins = A((acc if j == 0 else yb)[:, m, :], y_bank[:, m * T:(m + 1) * T], ACT.Identity,
                                bias=bias[:, HC + m:HC + m + 1], scale=UN / 2)
                    ins.then_inc(s_y, 1)

            def att(step, a):
                kind = step[0]
                if kind == "V":
                    act.wait_ge(s_qkv, 3 * a + 3)
                    wait(act, s_pv, 4 * a)
                    A(vp[:, :, :, 0:HEAD], bC[:].rearrange("p (t h e) -> p t h e", t=TT, h=NH), ACT.Copy
                      ).then_inc(s_v, 1)
                elif kind in ("TK", "TQ"):
                    first = 2 if kind == "TK" else 4 * step[1]
                    dst = kT if kind == "TK" else qT
                    if kind == "TK" or step[1] == 0:
                        wait(act, s_st, 16 * a)
                    else:
                        act.wait_ge(s_sn, 16 * a + 16)
                    for half in range(2):
                        act.wait_ge(s_tr, 6 * a + first + half + 1)
                        bank = ((bC, bA) if kind == "TK" else (bA, bB))[half]
                        A(dst[:, 4 * half:4 * half + 4, :], bank[:].bitcast(F16).rearrange("p (g t) -> p g t", g=4),
                          ACT.Copy).then_inc(s_te, 1)
                elif kind == "ST":
                    for h in (2 * step[1], 2 * step[1] + 1):
                        act.wait_ge(s_st, 16 * a + h + 1)
                        wait(act, s_pv, 4 * a + ((h - RING) // 4 + 1 if h >= RING else 0))
                        A(probs[:, h % RING, :, :], (bA, bB, bC)[h % 3][:].rearrange("p (k q) -> p k q", k=KC),
                          ACT.Exp).then_inc(s_exp, 1)
                elif kind == "PV" and step[1] % 2 == 1:
                    q = step[1] // 2
                    act.wait_ge(s_pv, 4 * a + step[1] + 1)
                    wait(act, s_on, 2 * a)
                    A(oT[:, 2 * q:2 * q + 2, :], bD[:].rearrange("p (n q) -> p n q", n=2), ACT.Copy
                      ).then_inc(s_oe, 1)
                elif kind == "AT":
                    act.wait_ge(s_at, a + 1)
                    wait(act, s_pp, a)
                    A(aT[:], bD[:].bitcast(F16).rearrange("p (n c t) -> p n c t", n=2, c=KC), ACT.Copy
                      ).then_inc(s_ate, 1)
                elif kind == "PJ":
                    act.wait_ge(s_xr, 16 * a + 16)
                    for m in range(KC):
                        ins = A(xr[:, m, :], xr[:, m, :], ACT.Identity, bias=pbias[:, m:m + 1])
                    ins.then_inc(s_xb, 1)

            def lstm(step, b):
                kind = step[0]
                if kind == "XW":
                    c, k = b - 2, step[1]
                    act.wait_ge(s_xp, 4 * c + k + 1)
                    if k == 0:
                        wait(act, s_pa, LT * c)
                    for m in range(2):
                        g = 2 * k + m
                        ins = A(xw[:, g], l1_bank[k % 2][:, m * T:(m + 1) * T].rearrange("p (t b) -> p t b", b=B),
                                ACT.Identity, bias=lbias[:, g:g + 1])
                    ins.then_inc(s_xe, 1)
                elif kind == "LS":
                    t = LT * (b - step[2]) + step[1]
                    act.wait_ge(s_pre, t + 1)
                    wait(act, s_hq, t)
                    A(uifo[:], pre[:, 0:6], ACT.Tanh, scale=UN / 2)
                    A(gcell[:, 0:2], pre[:, 6:8], ACT.Tanh, scale=UN).then_inc(s_sig, 1)
                elif kind == "LU":
                    t = LT * (b - step[2]) + step[1]
                    act.wait_ge(s_c, t + 1)
                    A(tanc[:], gcell[:, 2:4], ACT.Tanh, scale=0.5).then_inc(s_tc, 1)
                elif kind == "RS":
                    r = b - 3
                    act.wait_ge(s_r, r + 1)
                    act.wait_ge(s_acc, 2 * b if not isinstance(b, int) or b <= B else 2 * B)
                    act.wait_ge(s_rd, 16 * r + 16)
                    A(rbuf, y_bank[:], ACT.Copy, scale=UN).then_inc(s_re, 1)

            def emit(steps, b):
                for step in steps:
                    if step[0] in ("L1", "L2", "TH"):
                        moe(step, b)
                    elif step[0] in ("XW", "LS", "LU", "RS"):
                        lstm(step, b)
                    elif step[0] in ("ON", "AT", "PJ"):
                        att(step, b - 2)
                    else:
                        att(step, b - 1)

            phases(act, emit)

            def adapter_body(i):
                for n in range(2):
                    act.wait_ge(s_dn, 2 * i + n + 1)
                    wait(act, s_rs, 2 * i)
                    A(rl[:, n, :], banks[n][0:R, 0:T], ACT.Relu, scale=UN,
                      bias=hsel[0:R, n, EB - 2:EB].bitcast(F32)).then_inc(s_rl, 1)

            adapter_body(0)
            with act.Fori(1, B // 2) as i:
                adapter_body(i)

        @block.vector
        def _(dve):
            V = nc.vector
            UN = 1.0 / WSCALE
            chain = [0]

            def link(ins):
                chain[0] += 1
                ins.then_inc(s_set, 1)
                dve.wait_ge(s_set, chain[0])

            dve.wait_ge(s_const, 16 * len(consts))
            link(V.memset(adapt[R:P, :, 2 * KC * R:].bitcast(I32), 0))
            link(V.tensor_copy(ident16[:], ident[:]))
            link(V.tensor_scalar(ident64[:], ident[:], WSCALE, None, ALU.mult))
            for raw, dst in ((t1[0:33, :], brow_q[:, 0:512]), (t2[0:33, 0:256], brow_q[:, 512:768])):
                link(V.tensor_scalar(dst, raw, WSCALE, None, ALU.mult))
                link(V.scalar_tensor_tensor(dst[32:33], raw[32:33], WSCALE, dst[32:33], ALU.mult, ALU.subtract))
            link(V.tensor_scalar(lbias[:], lbias[:], WSCALE, None, ALU.mult))
            link(V.tensor_tensor(iv[:], sg[:], sg[:], ALU.mult))
            link(V.reciprocal(iv[:], iv[:]))
            link(V.tensor_tensor(mi2[:], mu[:], iv[:], ALU.mult))
            link(V.tensor_tensor(mmi[:], mu[:], mi2[:], ALU.mult))
            link(V.tensor_scalar(mi2[:], mi2[:], -2.0, None, ALU.mult))
            link(V.tensor_copy(adapt[0:R, :, EB - 2:EB].bitcast(F32), dbias[:].unsqueeze(2)))

            def cut(i):
                _, hi, lo, _, scale = chunks[i]
                dve.wait_ge(s_hi, i + 1)
                V.scalar_tensor_tensor(lo, match(stage(i), lo), scale, hi, ALU.mult, ALU.subtract).then_inc(s_lo, 1)

            def fold(e):
                dve.wait_ge(s_cp, e + 1)
                dve.wait_ge(s_cw, 64 * (e + 1))
                pw = bD[0:R + 1, 0:D]
                hi = adapt[0:R + 1, e, 2 * KC * R:2 * KC * R + D]
                lo = adapt[0:R + 1, e, 2 * KC * R + D:2 * KC * R + 2 * D]
                full = yb[0:R + 1, 0, :]
                link(V.tensor_copy(full, pw))
                link(V.tensor_tensor(cbrow[64:65, :], cbrow[64:65, :], t2[64:65, 0:D], ALU.add))
                link(V.tensor_tensor(yb[64:65, 0, :], yb[64:65, 0, :], cbrow[64:65, :], ALU.add))
                V.tensor_scalar(hi, full, WSCALE, None, ALU.mult).then_inc(s_cd, 1)
                dve.wait_ge(s_cd, 2 * e + 1)
                V.scalar_tensor_tensor(lo, full, WSCALE, hi, ALU.mult, ALU.subtract).then_inc(s_cd, 1)
                dve.wait_ge(s_cd, 2 * e + 2)

            for i in range(max(NCH, B)):
                if 3 <= i < 3 + EF:
                    fold(i - 3)
                if i < NCH:
                    cut(i)
                if i < B:
                    dve.wait_ge(s_gx[i % 2], 16 * (i // 2 + 1))
                    for n, (lo, hi) in enumerate(SEGS):
                        ins = V.tensor_reduce(sums[:, n, :, i:i + 1], (xt, xr)[i % 2][:, :, lo:hi], AX.X, ALU.add)
                    ins.then_inc(s_gsum, 1)
            dve.wait_ge(s_gsum, B)
            dve.wait_ge(s_ga, 1)
            link(V.tensor_scalar(small[:, 256:288], small[:, 256:288], 1.0, None, ALU.add))
            link(V.reciprocal(small[:, 256:288], small[:, 256:288]))
            link(V.tensor_tensor(small[:, 32:64], small[:, 0:32], small[:, 256:288], ALU.mult))
            hp, wp = T - LH, T - LH
            link(V.tensor_tensor(agg[:, 2:4], sums[:, 0], sums[:, 2], ALU.add))
            link(V.tensor_tensor(agg[:, 4:6], sums[:, 1], sums[:, 2], ALU.add))
            link(V.tensor_tensor(agg[:, 0:2], agg[:, 2:4], sums[:, 1], ALU.add))
            link(V.tensor_scalar(agg[:, 0:2], agg[:, 0:2], 1.0 / T, None, ALU.mult))
            link(V.tensor_scalar(agg[:, 2:6], agg[:, 2:6], 1.0 / hp, None, ALU.mult))
            assert chain[0] == GATE_READY, chain[0]
            lg, md, mx = route[:, 0:4], route[:, 4:12], route[:, 12:13]
            dve.wait_ge(s_gp, 1)
            link(V.tensor_tensor(lg, bA[0:B, 0:E], grow[:, 0:4], ALU.add))
            link(V.tensor_tensor(md, bB[0:B, 0:2 * E], grow[:, 4:12], ALU.add))
            link(V.scalar_tensor_tensor(lg, md[:, 0:4], 1.0, lg, ALU.add, ALU.mult))
            link(V.tensor_tensor(lg, lg, md[:, 4:8], ALU.add))
            link(V.tensor_reduce(mx, lg, AX.X, ALU.max, negate=True))
            assert chain[0] == LOGITS_READY, chain[0]
            dve.wait_ge(s_ga, 2)
            pr, rc = route[:, 16:20], route[:, 13:14]
            link(V.reciprocal(rc, rc))
            link(V.tensor_scalar(pr, pr, rc, None, ALU.mult))
            one, tmp = (route[:, 32:36], route[:, 36:40]), route[:, 40:44]
            best, pos = (route[:, 44:45], route[:, 45:46]), (route[:, 46:47], route[:, 47:48])
            for n in range(2):
                link(V.tensor_reduce(best[n], pr, AX.X, ALU.max))
                link(V.tensor_scalar(tmp, pr, best[n], None, ALU.is_ge))
                link(V.tensor_tensor(tmp, tmp, rev[:, 4:8], ALU.mult))
                link(V.tensor_reduce(pos[n], tmp, AX.X, ALU.max))
                link(V.tensor_scalar(one[n], rev[:, 4:8], pos[n], None, ALU.is_equal))
                if n == 0:
                    link(V.scalar_tensor_tensor(pr, one[0], -2.0, pr, ALU.mult, ALU.add))
            tot = route[:, 48:49]
            link(V.tensor_tensor(tot, best[0], best[1], ALU.add))
            link(V.tensor_scalar(tot, tot, 1e-8, None, ALU.add))
            link(V.reciprocal(tot, tot))
            row = route[:, 52:60]
            for n in range(2):
                w = row[:, 3 * n + 2:3 * n + 3]
                link(V.tensor_tensor(w, best[n], tot, ALU.mult))
                for s, masked in ((0, 2), (1, 1)):
                    f = row[:, 3 * n + s:3 * n + s + 1]
                    link(V.tensor_scalar(f, one[n][:, masked:masked + 1], -1.0, 1.0, ALU.mult, ALU.add))
                    link(V.tensor_tensor(f, f, w, ALU.mult))
                link(V.tensor_scalar(row[:, 6 + n:7 + n], pos[n], -1.0, float(E), ALU.mult, ALU.add))
            for n in range(8):
                ins = V.tensor_scalar(table[:, :, n], ident[0:B, 0:B], row[:, n:n + 1], None, ALU.mult)
            link(ins)
            assert chain[0] == TABLE_READY, chain[0]
            dve.wait_ge(s_gp, 2)
            link(V.tensor_copy(gates_b[:].rearrange("p b n -> p (b n)"), bC[:, 0:B * 8]))
            V.tensor_copy(idx_moe[:], gates_b[0:1, :, 6:8]).then_inc(s_idx, 1)
            assert chain[0] == SETUP_DONE, chain[0]

            def moe(step, b):
                kind, j = step[0:2]
                if kind != "AC":
                    g = step[2]
                    n = 12 * b + 4 * j + g
                    v, s2 = vb[:, g % 2, :], sq[:, (4 * j + g) % 3, :]
                if kind == "ZS":
                    dve.wait_ge(s_vs, n + 1)
                    V.scalar_tensor_tensor(s2, s2, GELU_C, v, ALU.add, ALU.mult).then_inc(s_z, 1)
                elif kind == "G2":
                    dve.wait_ge(s_th, n + 1)
                    V.scalar_tensor_tensor(s2, s2, 1.0, v, ALU.add, ALU.mult).then_inc(s_g2, 1)
                else:
                    u = 3 * b + j
                    if j >= 1:
                        dve.wait_ge(s_y, u + 1)
                        wait(dve, s_acc, 2 * b + j - 1)
                        for n, (lo, hi) in enumerate(SEGS):
                            w = gates_b[:, bass.ds(b, 1), 3 * (j - 1) + n]
                            ins = V.scalar_tensor_tensor(acc[:, :, lo:hi], yb[:, :, lo:hi], w, acc[:, :, lo:hi],
                                                         ALU.mult, ALU.add)
                        ins.then_inc(s_acc, 1)
                    if j == 2:
                        dve.wait_ge(s_acc, 2 * b + 2)
                        wait(dve, s_qkv, 3 * b)
                        V.tensor_copy(cs[:, 0], acc[:]).then_inc(s_ch, 1)
                        dve.wait_ge(s_ch, b + 1)
                        V.tensor_tensor(cs[:, 1], acc[:], cs[:, 0], ALU.subtract).then_inc(s_cs, 1)

            def att(step, a):
                kind = step[0]
                if kind == "QK":
                    tt = step[1]
                    dve.wait_ge(s_qkv, 3 * a + tt + 1)
                    wait(dve, s_qkn, 2 * a + tt)
                    base = 10 * a + 5 * tt
                    ps = (bA, bB)[tt]
                    psv, t1v, t2v = (x[:].rearrange("p (s h e) -> p s h e", s=2, e=HEAD) for x in (ps, t1, t2))
                    hw = HEAD // 2
                    lo_, hi_ = slice(0, hw), slice(hw, HEAD)

                    def all_heads(table, part, width):
                        return table[:, tt, :, part].unsqueeze(2).to_broadcast([P, 2, NH, width])

                    V.tensor_tensor(t1v, psv, all_heads(cos_t, slice(0, HEAD), HEAD), ALU.mult).then_inc(s_rp, 1)
                    V.tensor_tensor(t2v[:, :, :, lo_], psv[:, :, :, hi_], all_heads(sin_t, lo_, hw), ALU.mult
                                    ).then_inc(s_rp, 1)
                    V.tensor_tensor(t2v[:, :, :, hi_], psv[:, :, :, lo_], all_heads(sin_t, hi_, hw), ALU.mult
                                    ).then_inc(s_rp, 1)
                    dve.wait_ge(s_rp, base + 3)
                    V.tensor_tensor(t1[:], t1[:], t2[:], ALU.add).then_inc(s_rp, 1)
                    dve.wait_ge(s_rp, base + 4)
                    if tt == 0:
                        wait(dve, s_tr, 6 * a)
                    V.tensor_copy(qkn[:, tt, :, 0:16], t1[:].rearrange("p (h e) -> p h e", e=HEAD)).then_inc(s_rp, 1)
                elif kind == "SN":
                    for h in step[1]:
                        dve.wait_ge(s_sn, 16 * a + h + 1)
                        if h == 0:
                            wait(dve, s_mn, a)
                        bank = (bA, bB, bC)[h % 3]
                        V.tensor_reduce(mneg[:, :, h:h + 1], bank[:].rearrange("p (t k) -> p t k", t=TT), AX.X,
                                        ALU.max, negate=True).then_inc(s_mx, 1)
                    if step[1][-1] == NH - 1:
                        dve.wait_ge(s_mx, 16 * a + 16)
                        dve.wait_ge(s_tr, 6 * a + 4)
                        hi, lo = qkn[:, :, 0:NH, KSUM], qkn[:, :, 0:NH, KSUM + 1]
                        V.tensor_copy(hi, mneg[:]).then_inc(s_mh, 1)
                        dve.wait_ge(s_mh, a + 1)
                        V.tensor_tensor(lo, mneg[:], hi, ALU.subtract).then_inc(s_mn, 1)
                elif kind == "ON":
                    for tt in range(TT):
                        dve.wait_ge(s_on, 2 * a + tt + 1)
                        wait(dve, s_an, 2 * a + tt)
                        wait(dve, s_as, a)
                        o = (bA, bB)[tt][:].rearrange("p (h e) -> p h e", e=32)
                        V.reciprocal(recs[:, tt, :], o[:, :, HEAD]).then_inc(s_rc, 1)
                        dve.wait_ge(s_rc, 2 * a + tt + 1)
                        V.tensor_tensor(an[:, tt, :].rearrange("p (h e) -> p h e", e=HEAD), o[:, :, 0:HEAD],
                                        recs[:, tt, :].unsqueeze(2).to_broadcast([P, NH, HEAD]), ALU.mult
                                        ).then_inc(s_an, 1)
                elif kind == "AT":
                    dve.wait_ge(s_mi, 16 * B * (a + 1))
                    wait(dve, s_at, a)
                    V.tensor_copy(ah[:, 0], arow[:]).then_inc(s_ah, 1)
                    dve.wait_ge(s_ah, a + 1)
                    V.tensor_tensor(ah[:, 1], arow[:], ah[:, 0], ALU.subtract).then_inc(s_as, 1)
                elif kind == "PJ":
                    dve.wait_ge(s_pp, a + 1)
                    dve.wait_ge(s_xb, a + 1)
                    V.scalar_tensor_tensor(xr[:], bD[:].rearrange("p (c t) -> p c t", c=KC), UN, xr[:], ALU.mult,
                                           ALU.add).then_inc(s_xa, 1)
                    dve.wait_ge(s_xa, a + 1)
                    wait(dve, s_r, a)
                    V.tensor_copy(x2[:, 0], xr[:]).then_inc(s_xh, 1)
                    dve.wait_ge(s_xh, a + 1)
                    V.tensor_tensor(x2[:, 1], xr[:], x2[:, 0], ALU.subtract).then_inc(s_x2, 1)

            hb = h_bank[:, 0:GC * 2 * B].rearrange("p (g n) -> p g n", g=GC)

            def lstm_start():
                V.memset(gcell[:], 0.0)
                V.memset(stat[:], 0.0).then_inc(s_h0, 1)
                dve.wait_ge(s_h0, 1)
                V.tensor_scalar(hs[:, 0, :, LT - 1, :], condt, 2.0, None, ALU.mult).then_inc(s_h0, 1)
                dve.wait_ge(s_h0, 2)
                V.scalar_tensor_tensor(hs[:, 1, :, LT - 1, :], condt, 2.0, hs[:, 0, :, LT - 1, :], ALU.mult,
                                       ALU.subtract).then_inc(s_h, 1)

            def lstm(step, b):
                if step[0] != "SM":
                    s, c = step[1], b - step[2]
                    t = LT * c + s
                if step[0] == "LS":
                    if s == 0:
                        if isinstance(c, int) and c == 0:
                            lstm_start()
                        dve.wait_ge(s_xe, 4 * c + 4)
                        wait(dve, s_hist, c)
                        wait(dve, s_r, c)
                        wait(dve, s_sm, 4 * c)
                    dve.wait_ge(s_hp, t + 1)
                    V.tensor_tensor(pre[:], hb[:, :, 0:B], xw[:, :, s, :], ALU.add).then_inc(s_pa, 1)
                    dve.wait_ge(s_pa, t + 1)
                    V.tensor_tensor(pre[:], pre[:], hb[:, :, B:2 * B], ALU.add).then_inc(s_pre, 1)
                elif step[0] == "LC":
                    dve.wait_ge(s_sig, t + 1)
                    wait(dve, s_c, t)
                    V.scalar_tensor_tensor(prod[:], uifo[:, 0:4], 1.0, gcell[:], ALU.add, ALU.mult).then_inc(s_pr, 1)
                    dve.wait_ge(s_pr, t + 1)
                    V.scalar_tensor_tensor(gcell[:, 2:4], prod[:, 2:4], 0.5, prod[:, 0:2], ALU.mult, ALU.add
                                           ).then_inc(s_c, 1)
                elif step[0] == "LH":
                    dve.wait_ge(s_tc, t + 1)
                    V.scalar_tensor_tensor(hs[:, 0, :, s, :], uifo[:, 4:6], 1.0, tanc[:], ALU.add, ALU.mult)
                    V.scalar_tensor_tensor(hs_f[:, s], uifo[:, 4:6], 1.0, tanc[:], ALU.add, ALU.mult
                                           ).then_inc(s_hq, 1)
                    dve.wait_ge(s_hq, t + 1)
                    V.tensor_tensor(hs[:, 1, :, s, :], hs_f[:, s], hs[:, 0, :, s, :], ALU.subtract).then_inc(s_h, 1)
                else:
                    c = b - 3
                    by_t = hs_f[:].rearrange("p t c b -> p (c b) t")
                    dve.wait_ge(s_hq, LT * c + LT)
                    dve.wait_ge(s_h, LT * c + LT + 1)
                    V.tensor_reduce(stat[:, 0, :], by_t, AX.X, ALU.add).then_inc(s_sm, 1)
                    dve.wait_ge(s_sm, 4 * c + 1)
                    V.tensor_tensor(hs_f[:], hs_f[:], hs_f[:], ALU.mult).then_inc(s_sm, 1)
                    dve.wait_ge(s_sm, 4 * c + 2)
                    V.tensor_reduce(stat[:, 1, :], by_t, AX.X, ALU.add).then_inc(s_sm, 1)
                    dve.wait_ge(s_sm, 4 * c + 3)
                    V.tensor_tensor(stat[:, 2:4, :], stat[:, 2:4, :], stat[:, 0:2, :], ALU.add).then_inc(s_sm, 1)

            def emit(steps, b):
                for step in steps:
                    if step[0] in ("ZS", "G2", "AC"):
                        moe(step, b)
                    elif step[0] in ("LS", "LC", "LH", "SM"):
                        lstm(step, b)
                    elif step[0] in ("ON", "AT", "PJ"):
                        att(step, b - 2)
                    else:
                        att(step, b - 1)

            phases(dve, emit)

            fchain = [0]

            def flink(ins):
                fchain[0] += 1
                ins.then_inc(s_fd, 1)
                dve.wait_ge(s_fd, fchain[0])

            V.memset(rs_[R:R + 1, :, 0, :], 1.0)
            V.memset(rs_[R:R + 1, :, 1, :], 0.0)
            dve.wait_ge(s_sm, 4 * B)
            flink(V.tensor_scalar(stat[:, 2, :], stat[:, 2, :], 1.0 / (2 * T), None, ALU.mult))
            flink(V.tensor_scalar(stat[:, 3, :], stat[:, 3, :], 1.0 / (4 * T), None, ALU.mult))
            assert fchain[0] == STATS_READY
            dve.wait_ge(s_fl, 1)
            ls, tf = route[:, 0:8], route[:, 8:16]
            flink(V.tensor_scalar(ls, bA[0:B, 0:EF], -1.0 / D, None, ALU.mult))
            flink(V.tensor_reduce(route[:, 25:26], ls, AX.X, ALU.max))
            flink(V.tensor_scalar(tf, ls, route[:, 25:26], None, ALU.is_ge))
            flink(V.tensor_tensor(tf, tf, rev[:], ALU.mult))
            flink(V.tensor_reduce(route[:, 26:27], tf, AX.X, ALU.max))
            flink(V.tensor_scalar(route[:, 24:25], route[:, 26:27], -1.0, float(EF), ALU.mult, ALU.add))
            assert fchain[0] == INDEX_READY
            dve.wait_ge(s_fl, 2)
            flink(V.tensor_copy(idx_ffn[:], bB[0:1, 0:B]))

            def adapter_body(i):
                start = isinstance(i, int)
                for pair in range(2):
                    for n in range(2):
                        b = 4 * i + 2 * pair + n
                        if not (start and pair == 0):
                            dve.wait_ge(s_fo, b - 1)
                        e = dve.value_load(idx_ffn[0:1, bass.ds(b, 1)], min_val=0, max_val=EF - 1)
                        V.tensor_copy(hsel[:, n, :].bitcast(I32).unsqueeze(1),
                                      adapt_in.bitcast(I32)[:, bass.ds(e, 1), :]).then_inc(s_sel, 1)
                    for n in range(2):
                        b = 4 * i + 2 * pair + n
                        dve.wait_ge(s_rl, b + 1)
                        V.tensor_copy(rs_[0:R, n, 0, :], rl[:, n, :]).then_inc(s_rh, 1)
                        dve.wait_ge(s_rh, b + 1)
                        V.tensor_tensor(rs_[0:R, n, 1, :], rl[:, n, :], rs_[0:R, n, 0, :], ALU.subtract
                                        ).then_inc(s_rs, 1)
                    for n in range(2):
                        b = 4 * i + 2 * pair + n
                        dve.wait_ge(s_fo, b + 1)
                        dve.wait_ge(s_rin[2 * pair + n], 16 * i + 16)
                        if not (start and pair == 0):
                            dve.wait_ge(s_out[n], 32 * i + 16 * pair)
                        V.scalar_tensor_tensor(obuf[:, n, :], banks[4 + n][:], UN, rin[:, 2 * pair + n, :], ALU.mult,
                                               ALU.add).then_inc(s_ob, 1)

            dve.wait_ge(s_ain, 16)
            adapter_body(0)
            with dve.Fori(1, B // 4) as i:
                adapter_body(i)


def kernel(**inputs):
    import numpy as np
    import concourse.bacc as _bacc
    from concourse import mybir as _mybir
    from concourse.bass_utils import run_bass_kernel_spmd as _run

    v = {k: np.asarray(a) for k, a in inputs.items()}
    con = np.ascontiguousarray

    def cols(a, c):
        return con(a.reshape((c, P) + a.shape[1:]).swapaxes(0, 1))

    pos = np.arange(256, dtype=np.float32)
    inv = (1.0 / 10000.0 ** (np.arange(0, HEAD, 2, dtype=np.float32) / np.float32(HEAD))).astype(np.float32)
    ang = (pos[:, None] * inv[None, :]).astype(np.float32)
    cos = np.concatenate([np.cos(ang), np.cos(ang)], -1).astype(np.float32)
    sin = np.concatenate([-np.sin(ang), np.sin(ang)], -1).astype(np.float32)
    scale_q, scale_k = np.float32(HEAD ** -0.5 / WSCALE), np.float32(1.0 / WSCALE)

    def rotary(t):
        return cols(np.stack([t * scale_q, t * scale_k], 1), 2)

    eb = np.concatenate([v["L0_cond_eb1"].reshape(4, 8, P).swapaxes(1, 2),
                         v["L0_cond_eb2"].reshape(4, 2, P).swapaxes(1, 2)], 2)
    sbias = np.concatenate([v["L0_cond_sb1"].reshape(8, P).T, v["L0_cond_sb2"].reshape(2, P).T], 1)
    up = np.concatenate([v["L0_ffn_up_W"].transpose(0, 2, 1), v["L0_ffn_up_b"][:, :, None]], 2)
    arrays = {
        "xT": v["x"].transpose(0, 2, 1).reshape(16, 2, P, 256).transpose(0, 2, 1, 3),
        "xL": v["x"].reshape(16, 16, 16, 2, P).transpose(1, 4, 3, 2, 0).reshape(16, P, 2, 256),
        "condT": cols(v["cond_1024"].T, 2),
        "gw": cols(v["L0_cond_gate_w"], 6), "tw": cols(v["L0_cond_time_w"], 2),
        "grow": np.concatenate([v["L0_cond_gate_b"], v["L0_cond_time_b"]]),
        "ew1": v["L0_cond_ew1"], "ew2": v["L0_cond_ew2"], "sw1": v["L0_cond_sw1"], "sw2": v["L0_cond_sw2"],
        "ebias": eb, "sbias": sbias,
        "qkvT": v["L0_attn_qkv_w"].T, "qb": v["L0_attn_qkv_b"][None], "projT": v["L0_attn_proj_w"].T,
        "pbias": v["L0_attn_proj_b"].reshape(2, P).T,
        "wx": v["L0_cond2_Wx"], "wh": v["L0_cond2_Wh"], "lb": v["L0_cond2_b"].reshape(8, P).T,
        "baseT": v["L0_ffn_base_W"].T, "bb": v["L0_ffn_base_b"][None],
        "muT": cols(v["L0_ffn_disc_mu"].T, 2), "sgT": cols(v["L0_ffn_disc_sigma"].T, 2),
        "downT": v["L0_ffn_down_W"].reshape(8, 2, P, 64).transpose(2, 0, 1, 3).reshape(P, 8, 128),
        "downbT": v["L0_ffn_down_b"].T,
        "upT": up.reshape(8, 2, P, 65).swapaxes(1, 2),
        "convT": v["L0_ffn_conv_W"].transpose(0, 2, 1).reshape(8, 2, P, 256).swapaxes(1, 2),
        "cb": v["L0_ffn_conv_b"],
        "ident": np.eye(P, dtype=np.float32), "rev": np.arange(8, 0, -1).astype(np.float32),
        "cos_t": rotary(cos), "sin_t": rotary(sin),
    }
    arrays = {k: con(a) for k, a in arrays.items()}
    nc = _bacc.Bacc("TRN2", target_bir_lowering=False, num_devices=1)
    d = {k: nc.dram_tensor(f"in_{k}", a.shape, _mybir.dt.from_np(a.dtype), kind="ExternalInput").ap()
         for k, a in arrays.items()}
    d["out"] = nc.dram_tensor("out_y", (16, 256, 256), _mybir.dt.float32, kind="ExternalOutput").ap()
    mixer_kernel(nc, d)
    r = _run(nc, [{f"in_{k}": a for k, a in arrays.items()}], core_ids=[0])
    return r.results[0]["out_y"]
```
